# Optimizing a Trainium2 kernel written in Bass

```python
import numpy as np
import jax
import jax.numpy as jnp

def _softmax(x, axis=-1):
    return jax.nn.softmax(x, axis=axis)

def _gelu(x):
    return jax.nn.gelu(x, approximate=True)

def _silu(x):
    return jax.nn.silu(x)

def _sigmoid(x):
    return jax.nn.sigmoid(x)

def _layernorm(x, axis=-1, eps=1e-05):
    m = jnp.mean(x, axis=axis, keepdims=True)
    v = jnp.var(x, axis=axis, keepdims=True)
    return (x - m) / jnp.sqrt(v + eps)

def _scatter_add(tgt, idx, src, axis=0):
    return tgt.at[idx].add(src)

def _segment_sum(src, seg, n):
    return jax.ops.segment_sum(src, seg, n)
kernel_name = 'mk_adj_ffn_d1_adj_r2_2548f5'

def setup_inputs(seed: int=0):
    np.random.seed(seed)
    _w = jnp.asarray

    def _rec_inputs():
        import jax
        import jax.numpy as jnp
        _gk = jax.random.key(seed)
        x = -0.0002928 + 1 * jax.random.normal(jax.random.fold_in(_gk, 1), (8192, 128), jnp.float32)
        _w = (1.0 + jnp.arange(8192, dtype=jnp.float32)) ** (-0.5)
        _w = _w / _w.mean()
        _pij = jnp.clip(0.000488281 * _w[:, None] * _w[None, :], 0.0, 1.0)
        _a = jax.random.uniform(jax.random.fold_in(_gk, 2), (8192, 8192)) < _pij
        _a = jnp.logical_or(_a, jnp.eye(8192, dtype=bool))
        _af = _a.astype(jnp.float32)
        _af = _af * jax.random.uniform(jax.random.fold_in(_gk, 3), (8192, 8192), jnp.float32, 0.05, 6.10351e-05)
        adj = _af
        return (x, adj)
    x, adj = _rec_inputs()

    def _L0_gnn_setup():
        import jax, jax.numpy as jnp
        import numpy as np
        N_NODES = 8192
        D_FEAT = 128
        key = jax.random.key(seed)
        k1, k2, k3, k4 = jax.random.split(key, 4)
        X = jax.random.normal(k1, (N_NODES, D_FEAT), dtype=jnp.float32)
        A_hat = jax.random.uniform(k2, (N_NODES, N_NODES), dtype=jnp.float32) / N_NODES
        w = jax.random.uniform(k3, (N_NODES,), dtype=jnp.float32)
        W_agg = jax.random.normal(k4, (D_FEAT, D_FEAT), dtype=jnp.float32) / np.sqrt(D_FEAT)
        return {'X': X, 'A_hat': A_hat, 'w': w, 'W_agg': W_agg}
    _L0_gnn_all = _L0_gnn_setup()
    _L0_gnn_in = {k: v for k, v in _L0_gnn_all.items() if k in ('w', 'W_agg')}
    del _L0_gnn_all

    def _L0_ffn_setup():
        import jax, jax.numpy as jnp
        import numpy as np
        C = 128
        HID = 512
        E = 8
        TEMP = 1.0
        key = jax.random.key(seed)
        ks = jax.random.split(key, 7)
        x = jax.random.normal(ks[0], (8, 8192, C), dtype=jnp.float32)
        W1 = jax.random.normal(ks[1], (C, HID), dtype=jnp.float32) * 0.02
        b1 = jnp.zeros((HID,), dtype=jnp.float32)
        Wg = jax.random.normal(ks[2], (HID, E), dtype=jnp.float32) * 0.02
        bg = jnp.zeros((E,), dtype=jnp.float32)
        Wd = jax.random.normal(ks[3], (E, HID, C), dtype=jnp.float32) * 0.02
        bd = jnp.zeros((E, C), dtype=jnp.float32)
        return {'x': x, 'W1': W1, 'b1': b1, 'Wg': Wg, 'bg': bg, 'Wd': Wd, 'bd': bd}
    _L0_ffn_all = _L0_ffn_setup()
    _L0_ffn_in = {k: v for k, v in _L0_ffn_all.items() if k in ('W1', 'b1', 'Wg', 'bg', 'Wd', 'bd')}
    del _L0_ffn_all
    return {'x': x, 'adj': adj, 'L0_gnn_w': _L0_gnn_in['w'], 'L0_gnn_W_agg': _L0_gnn_in['W_agg'], 'L0_ffn_W1': _L0_ffn_in['W1'], 'L0_ffn_b1': _L0_ffn_in['b1'], 'L0_ffn_Wg': _L0_ffn_in['Wg'], 'L0_ffn_bg': _L0_ffn_in['bg'], 'L0_ffn_Wd': _L0_ffn_in['Wd'], 'L0_ffn_bd': _L0_ffn_in['bd']}

def reference(x, adj, L0_gnn_w, L0_gnn_W_agg, L0_ffn_W1, L0_ffn_b1, L0_ffn_Wg, L0_ffn_bg, L0_ffn_Wd, L0_ffn_bd):
    import jax
    import jax.numpy as jnp

    def _L0_gnn_ref(X, A_hat, w, W_agg):
        import jax, jax.numpy as jnp
        import numpy as np
        N_NODES = 8192
        D_FEAT = 128
        agg = jnp.matmul(jnp.matmul(A_hat, X), W_agg)
        agg = jax.nn.relu(agg)
        s = jax.nn.sigmoid(w)[:, None]
        return s * agg + (1.0 - s) * X

    def _L0_ffn_ref(x, W1, b1, Wg, bg, Wd, bd):
        import jax, jax.numpy as jnp
        import numpy as np
        C = 128
        HID = 512
        E = 8
        TEMP = 1.0
        orig_shape = x.shape
        xf = x.reshape(-1, orig_shape[-1])
        H = jax.nn.gelu(xf @ W1 + b1, approximate=False)
        probs = jax.nn.softmax((H @ Wg + bg) / TEMP, axis=-1)
        assign = jnp.argmax(probs, axis=-1)
        out = jnp.zeros_like(xf)
        for e in range(Wd.shape[0]):
            y = H @ Wd[e] + bd[e]
            sel = (assign == e)[:, None]
            out = out + jnp.where(sel, probs[:, e:e + 1] * y, 0.0)
        return out.reshape(orig_shape)
    x = x + _L0_gnn_ref(_layernorm(x, axis=-1), adj, L0_gnn_w, L0_gnn_W_agg)
    x = x + _L0_ffn_ref(_layernorm(x, axis=-1)[None], L0_ffn_W1, L0_ffn_b1, L0_ffn_Wg, L0_ffn_bg, L0_ffn_Wd, L0_ffn_bd)[0]
    return x

_drawn_inputs = setup_inputs


def setup_inputs(seed=0):
    import zlib

    import numpy as np

    out = dict(_drawn_inputs(seed))
    spreads = {'L0_ffn_b1': (0.0, 0.8), 'L0_ffn_bg': (0.0, 0.594), 'L0_ffn_bd': (0.0, 0.8)}
    factors = {'L0_ffn_W1': 6.929, 'L0_ffn_Wg': 6.729, 'L0_ffn_Wd': 8.0}
    for name, (base, spread) in spreads.items():
        noise = np.random.default_rng([zlib.crc32(name.encode()), seed]).standard_normal(out[name].shape)
        drawn = base * np.exp(spread * noise) if base else spread * noise
        out[name] = jnp.asarray(drawn.astype(out[name].dtype))
    for name, factor in factors.items():
        out[name] = (out[name] * factor).astype(out[name].dtype)
    return out
```

```python
from contextlib import ExitStack

import concourse.bass as bass
from concourse import mybir

F32 = mybir.dt.float32
F32R = mybir.dt.float32r
ALU = mybir.AluOpType
ACT = mybir.ActivationFunctionType
AX = mybir.AxisListType

P = 128
N = 8192
C = 128
HID = 512
E = 8
BLOCK = 512
BLOCKS = N // BLOCK
TILES = N // P
TPB = BLOCK // P
JB = 2
CHUNKS = TILES // JB
RAW = 4
RING = 2
HC = HID // P
GT = 8
GROUPS = TILES // GT
CPG = GT // JB
EPS = 1e-5

AT_X1T, AT_XNT, AT_H, AT_LT, AT_CT, AT_BD, AT_Y = 1, 5, 7, 12, 15, 16, 17
H_STEP, Y_STEP = 1, 4


def build(nc, x, adj, w, W_agg, W1, b1, Wg, bg, Wd, bd, ident, rank, out):
    with ExitStack() as ctx:
        def sb(name, shape, dt=F32):
            return ctx.enter_context(nc.sbuf_tensor(name, shape, dt))

        def bank(name):
            return ctx.enter_context(nc.psum_tensor(name, [P, BLOCK], F32))

        def sem(name):
            return ctx.enter_context(nc.semaphore(name))

        xw_hi = sb("xw_hi", [P, TILES, C], F32R)
        xw_lo = sb("xw_lo", [P, TILES, C], F32R)
        base = sb("base", [P, TILES, C])
        wd_hi = sb("wd_hi", [P, HC, E * C], F32R)
        wd_lo = sb("wd_lo", [P, HC, E * C], F32R)
        w1_hi = sb("w1_hi", [P, HID], F32R)
        w1_lo = sb("w1_lo", [P, HID], F32R)
        wagg = sb("wagg", [P, C])
        wg = sb("wg", [P, HC, E])
        b1c = sb("b1c", [P, HC])
        bgb = sb("bgb", [P, E])
        bdr = sb("bdr", [E, C])
        idn = sb("idn", [P, P])
        rnk = sb("rnk", [P, E])
        wcol = sb("wcol", [P, TILES])
        s = sb("s", [P, TILES])
        s1m = sb("s1m", [P, TILES])
        raw = sb("raw", [P, RAW, JB, BLOCK])
        a_hi = sb("a_hi", [P, RING, JB, BLOCK], F32R)
        a_lo = sb("a_lo", [P, RING, JB, BLOCK], F32R)
        h_f = sb("h_f", [P, 2, BLOCK])
        tmp = sb("tmp", [P, 2, BLOCK])
        x1 = sb("x1", [P, TPB, C])
        xnt_hi = sb("xnt_hi", [P, BLOCK], F32R)
        xnt_lo = sb("xnt_lo", [P, BLOCK], F32R)
        h_hi = sb("h_hi", [P, HC, BLOCK], F32R)
        h_lo = sb("h_lo", [P, HC, BLOCK], F32R)
        lct = sb("lct", [E, BLOCK])
        half = sb("half", [P, GT])
        eps = sb("eps", [P, GT])
        st = sb("st", [P, GT, 6])
        mv = sb("mv", [P, GT, 2])
        veps = sb("veps", [P, GT])
        rstd = sb("rstd", [P, GT])
        lg = sb("lg", [P, TPB, E])
        zz = sb("zz", [P, TPB, E])
        th = sb("th", [P, TPB, E])
        dn = sb("dn", [P, TPB, E])
        ex = sb("ex", [P, TPB, E])
        eq = sb("eq", [P, TPB, E])
        cf = sb("cf", [P, TPB, E])
        mx = sb("mx", [P, TPB])
        sm = sb("sm", [P, TPB])
        pr = sb("pr", [P, TPB])
        fi = sb("fi", [P, TPB])

        agg = bank("agg")
        tb = bank("tb")
        hb = [bank("hb0"), bank("hb1")]
        yb = [bank("yb0"), bank("yb1")]
        lb = bank("lb")
        zb = bank("zb")

        relu_t, xn2 = tmp[:, 0, :], tmp[:, 1, :]
        x_t = tmp
        xn = [h_f, x1]

        x_in = [sem(f"x_in{g}") for g in range(GROUPS)]
        small_in = sem("small_in")
        s_done = sem("s_done")
        s1m_done = sem("s1m_done")
        half_done = sem("half_done")
        su_st = sem("su_st")
        su_aggr = sem("su_aggr")
        su_mv = sem("su_mv")
        su_veps = sem("su_veps")
        su_rstd = sem("su_rstd")
        su_xn = sem("su_xn")
        su_tr = sem("su_tr")
        su_xt = sem("su_xt")
        su_xw = sem("su_xw")
        su_hi = sem("su_hi")
        su_lo = sem("su_lo")
        su_res = sem("su_res")
        su_base = sem("su_base")
        w_in = sem("w_in")
        w_hi = sem("w_hi")
        w_lo = sem("w_lo")
        raw_in = [sem(f"raw_in{r}") for r in range(RAW)]
        adj_hi = sem("adj_hi")
        adj_lo = sem("adj_lo")
        adj_mm = sem("adj_mm")
        relu_done = sem("relu_done")
        x1t_ready = sem("x1t_ready")
        x1_done = sem("x1_done")
        st_done = sem("st_done")
        aggr_done = sem("aggr_done")
        mv_done = sem("mv_done")
        veps_done = sem("veps_done")
        rstd_done = sem("rstd_done")
        xn_done = sem("xn_done")
        xnt_ready = sem("xnt_ready")
        xnt_hi_done = sem("xnt_hi_done")
        xnt_lo_done = sem("xnt_lo_done")
        h_ready = sem("h_ready")
        gelu_done = sem("gelu_done")
        h_hi_done = sem("h_hi_done")
        h_lo_done = sem("h_lo_done")
        logit_mm = sem("logit_mm")
        lt_done = sem("lt_done")
        logits_ready = sem("logits_ready")
        z_done = sem("z_done")
        tanh_done = sem("tanh_done")
        soft = sem("soft")
        eq_done = sem("eq_done")
        coef_done = sem("coef_done")
        ct_ready = sem("ct_ready")
        ct_done = sem("ct_done")
        bd_ready = sem("bd_ready")
        bd_done = sem("bd_done")
        y_ready = sem("y_ready")
        comb = sem("comb")
        y_used = sem("y_used")
        out_done = sem("out_done")
        SOFT = 10

        block = ctx.enter_context(nc.Block())

        @block.sync
        def _(sp):
            def load(B, c):
                nc.sync.dma_start(raw[:, c % RAW], adj[B, c]).then_inc(raw_in[c % RAW], 16)

            for g in range(GROUPS):
                nc.sync.dma_start(base[:, g * GT:(g + 1) * GT, :], x[:, g * GT:(g + 1) * GT, :]
                                  ).then_inc(x_in[g], 16)
                for c in range(g * CPG, (g + 1) * CPG):
                    if c >= RAW:
                        sp.wait_ge(adj_lo, c - RAW + 1)
                    load(0, c)
            with sp.Fori(1, BLOCKS) as B:
                for c in range(CHUNKS):
                    sp.wait_ge(adj_lo, B * CHUNKS + (c - RAW + 1))
                    load(B, c)

        @block.gpsimd
        def _(pool):
            nc.gpsimd.memset(half[:], -0.5).then_inc(half_done, 1)
            nc.gpsimd.memset(eps[:], EPS).then_inc(half_done, 1)
            pool.wait_ge(half_done, 2)
            for g in range(GROUPS):
                pool.wait_ge(su_mv, g + 1)
                nc.gpsimd.tensor_tensor(veps[:], mv[:, :, 1], eps[:], ALU.add).then_inc(su_veps, 1)
                pool.wait_ge(su_veps, g + 1)
                nc.gpsimd.tensor_tensor(rstd[:], veps[:], half[:], ALU.pow).then_inc(su_rstd, 1)
                if g == 0:
                    pool.wait_ge(s1m_done, 1)
                for u in range(2):
                    t0 = g * GT + u * TPB
                    xn_u = xn[u][:] if u else xn[u][:].rearrange("p a (b c) -> p (a b) c", c=C)[:, 0:TPB, :]
                    pool.wait_ge(su_tr, 2 * g + u + 1)
                    nc.gpsimd.tensor_tensor(
                        xn_u, xn_u, s1m[:, t0:t0 + TPB].unsqueeze(2).to_broadcast([P, TPB, C]),
                        ALU.mult).then_inc(su_res, 1)
                    pool.wait_ge(su_res, 2 * g + u + 1)
                    nc.gpsimd.tensor_tensor(base[:, t0:t0 + TPB, :], base[:, t0:t0 + TPB, :], xn_u,
                                            ALU.add).then_inc(su_base, 1)

            def ffn(b):
                pool.wait_ge(mv_done, b + 1)
                nc.gpsimd.tensor_tensor(veps[:, 0:TPB], mv[:, 0:TPB, 1], eps[:, 0:TPB], ALU.add
                                        ).then_inc(veps_done, 1)
                pool.wait_ge(veps_done, b + 1)
                nc.gpsimd.tensor_tensor(rstd[:, 0:TPB], veps[:, 0:TPB], half[:, 0:TPB], ALU.pow
                                        ).then_inc(rstd_done, 1)

            ffn(0)
            with pool.Fori(1, BLOCKS) as b:
                ffn(b)

        @block.scalar
        def _(act):
            smalls = [(wcol, w), (wagg, W_agg), (idn, ident), (wg, Wg), (b1c, b1), (bgb, bg), (bdr, bd),
                      (rnk, rank)]
            for dst, src in smalls:
                nc.scalar.dma_start(dst[:], src).then_inc(small_in, 16)
            act.wait_ge(small_in, 16 * len(smalls))
            nc.scalar.activation(s[:], wcol[:], ACT.Sigmoid).then_inc(s_done, 1)

            def split(B, c, first=False):
                act.wait_ge(raw_in[c % RAW], B * (16 * CHUNKS // RAW) + 16 * (c // RAW + 1))
                if not (first and c < RING):
                    act.wait_ge(adj_mm, B * CHUNKS + (c - RING + 1))
                nc.scalar.activation(a_hi[:, c % RING], raw[:, c % RAW], ACT.Copy).then_inc(adj_hi, 1)

            def setup(g):
                for u in range(2):
                    act.wait_ge(su_tr, 2 * g + u + 1)
                    nc.scalar.copy(x_t[:, u, :], hb[u][:]).then_inc(su_xt, 1)
                for u in range(2):
                    t0 = g * GT + u * TPB
                    act.wait_ge(su_xw, 2 * g + u + 1)
                    nc.scalar.activation(xw_hi[:, t0:t0 + TPB, :], yb[u][:], ACT.Copy).then_inc(su_hi, 1)

            setup(0)
            for c in range(CHUNKS):
                split(0, c, True)
                if c % CPG == 1 and c // CPG + 1 < GROUPS:
                    setup(c // CPG + 1)
            stage = x1[:].rearrange("p a b -> p (a b)")
            pieces = [(W1, w1_hi[:])] + [
                (Wd[h, :, u * BLOCK:(u + 1) * BLOCK], wd_hi[:, h, u * BLOCK:(u + 1) * BLOCK])
                for h in range(HC) for u in range(2)]
            act.wait_ge(su_base, 2 * GROUPS)
            for n, (src, hi) in enumerate(pieces):
                if n:
                    act.wait_ge(w_lo, n)
                nc.scalar.dma_start(stage, src).then_inc(w_in, 16)
                act.wait_ge(w_in, 16 * (n + 1))
                nc.scalar.activation(hi, stage, ACT.Copy).then_inc(w_hi, 1)

            def step(b, B):
                def chunks(lo, hi):
                    if B is not None:
                        for c in range(lo, hi):
                            split(B, c)

                chunks(0, RING)
                act.wait_ge(adj_mm, b * CHUNKS + CHUNKS)
                nc.scalar.activation(relu_t, agg[:], ACT.Relu).then_inc(relu_done, 1)
                chunks(RING, AT_XNT + 2)
                act.wait_ge(xnt_ready, b + 1)
                nc.scalar.activation(xnt_hi[:], tb[:], ACT.Copy).then_inc(xnt_hi_done, 1)
                chunks(AT_XNT + 2, AT_H + 1)
                for h in range(HC):
                    act.wait_ge(h_ready, b * HC + (h + 1))
                    if h >= 2:
                        act.wait_ge(h_lo_done, b * HC + (h - 1))
                        act.wait_ge(logit_mm, b * HC + (h - 1))
                    nc.scalar.activation(h_f[:, h % 2, :], hb[h % 2][:], ACT.Gelu,
                                         bias=b1c[:, h:h + 1]).then_inc(gelu_done, 1)
                    act.wait_ge(gelu_done, b * HC + (h + 1))
                    nc.scalar.activation(h_hi[:, h, :], h_f[:, h % 2, :], ACT.Copy).then_inc(h_hi_done, 1)
                    chunks(AT_H + 1 + h, AT_H + 2 + h)
                chunks(AT_H + HC + 1, AT_LT)
                act.wait_ge(logit_mm, b * HC + HC)
                nc.scalar.copy(lct[:], lb[0:E, :]).then_inc(lt_done, 1)
                chunks(AT_LT, AT_LT + 2)
                act.wait_ge(z_done, b + 1)
                nc.scalar.activation(th[:], zz[:], ACT.Tanh, scale=0.5).then_inc(tanh_done, 1)
                chunks(AT_LT + 2, AT_CT + 1)
                act.wait_ge(ct_ready, b + 1)
                nc.scalar.copy(lct[:], zb[0:E, :]).then_inc(ct_done, 1)
                chunks(AT_CT + 1, CHUNKS)
                act.wait_ge(y_used, b * TPB + TPB)
                nc.scalar.dma_start(out[b], x1[:]).then_inc(out_done, 16)

            step(0, 1)
            with act.Fori(1, BLOCKS - 1) as b:
                step(b, b + 1)
            step(BLOCKS - 1, None)
            act.wait_ge(out_done, 16 * BLOCKS)

        @block.vector
        def _(dve):
            dve.wait_ge(s_done, 1)
            nc.vector.tensor_scalar(s1m[:], s[:], -1.0, 1.0, ALU.mult, ALU.add).then_inc(s1m_done, 1)

            def split(B, c):
                dve.wait_ge(adj_hi, B * CHUNKS + (c + 1))
                nc.vector.tensor_tensor(a_lo[:, c % RING], raw[:, c % RAW], a_hi[:, c % RING].bitcast(F32),
                                        ALU.subtract).then_inc(adj_lo, 1)

            def normalise(g):
                dve.wait_ge(x_in[g], 16)
                for t in range(GT):
                    nc.vector.bn_stats(st[:, t, :], base[:, g * GT + t, :]).then_inc(su_st, 1)
                if g:
                    dve.wait_ge(su_veps, g)
                for t in range(GT):
                    dve.wait_ge(su_st, g * GT + t + 1)
                    last = nc.vector.bn_aggr(mv[:, t, :], st[:, t, :])
                    if t < GT - 1:
                        last.then_inc(su_aggr, 1)
                last.then_inc(su_mv, 1)
                dve.wait_ge(su_aggr, (g + 1) * (GT - 1))
                dve.wait_ge(su_mv, g + 1)
                dve.wait_ge(su_rstd, g + 1)
                if g:
                    dve.wait_ge(su_base, 2 * g)
                for t in range(GT):
                    u, v = t // TPB, t % TPB
                    dst = x1[:, v, :] if u else h_f[:].rearrange("p a (b c) -> p (a b) c", c=C)[:, v, :]
                    nc.vector.tensor_scalar(dst, base[:, g * GT + t, :], mv[:, t, 0:1], rstd[:, t:t + 1],
                                            ALU.subtract, ALU.mult).then_inc(su_xn, 1)

            def low(g):
                for u in range(2):
                    t0 = g * GT + u * TPB
                    dve.wait_ge(su_hi, 2 * g + u + 1)
                    nc.vector.tensor_tensor(xw_lo[:, t0:t0 + TPB, :], yb[u][:].rearrange("p (a b) -> p a b", b=C),
                                            xw_hi[:, t0:t0 + TPB, :].bitcast(F32), ALU.subtract
                                            ).then_inc(su_lo, 1)

            normalise(0)
            low(0)
            for c in range(CHUNKS):
                if c % CPG == 0 and c // CPG + 1 < GROUPS:
                    normalise(c // CPG + 1)
                split(0, c)
                if c % CPG == 1 and c // CPG + 1 < GROUPS:
                    low(c // CPG + 1)
            stage = x1[:].rearrange("p a b -> p (a b)")
            pieces = [(w1_lo[:], w1_hi[:])] + [
                (wd_lo[:, h, u * BLOCK:(u + 1) * BLOCK], wd_hi[:, h, u * BLOCK:(u + 1) * BLOCK])
                for h in range(HC) for u in range(2)]
            for n, (lo, hi) in enumerate(pieces):
                dve.wait_ge(w_hi, n + 1)
                nc.vector.tensor_tensor(lo, stage, hi.bitcast(F32), ALU.subtract).then_inc(w_lo, 1)

            def step(b, B, first=False):
                def chunks(lo, hi):
                    if B is not None:
                        for c in range(lo, hi):
                            split(B, c)

                chunks(0, AT_X1T + 2)
                dve.wait_ge(x1t_ready, b + 1)
                if not first:
                    dve.wait_ge(out_done, b * 16)
                for k in range(TPB):
                    nc.vector.scalar_tensor_tensor(
                        x1[:, k, :], tb[:, k * C:(k + 1) * C], s[:, bass.ds(b * TPB + k, 1)],
                        base[:, bass.ds(b * TPB + k, 1), :].rearrange("p a c -> p (a c)"),
                        ALU.mult, ALU.add).then_inc(x1_done, 1)
                for k in range(TPB):
                    dve.wait_ge(x1_done, b * TPB + (k + 1))
                    nc.vector.bn_stats(st[:, k, :], x1[:, k, :]).then_inc(st_done, 1)
                dve.wait_ge(st_done, b * TPB + TPB)
                chunks(AT_X1T + 2, AT_X1T + 3)
                for k in range(TPB):
                    last = nc.vector.bn_aggr(mv[:, k, :], st[:, k, :])
                    if k < TPB - 1:
                        last.then_inc(aggr_done, 1)
                last.then_inc(mv_done, 1)
                chunks(AT_X1T + 3, AT_X1T + 4)
                dve.wait_ge(aggr_done, b * (TPB - 1) + (TPB - 1))
                dve.wait_ge(rstd_done, b + 1)
                for k in range(TPB):
                    nc.vector.tensor_scalar(xn2[:, k * C:(k + 1) * C], x1[:, k, :], mv[:, k, 0:1],
                                            rstd[:, k:k + 1], ALU.subtract, ALU.mult).then_inc(xn_done, 1)
                chunks(AT_X1T + 4, AT_XNT + 2)
                dve.wait_ge(xnt_hi_done, b + 1)
                nc.vector.tensor_tensor(xnt_lo[:], tb[:], xnt_hi[:].bitcast(F32), ALU.subtract
                                        ).then_inc(xnt_lo_done, 1)
                chunks(AT_XNT + 2, AT_H + 1)
                for h in range(HC):
                    dve.wait_ge(h_hi_done, b * HC + (h + 1))
                    nc.vector.tensor_tensor(h_lo[:, h, :], h_f[:, h % 2, :], h_hi[:, h, :].bitcast(F32),
                                            ALU.subtract).then_inc(h_lo_done, 1)
                    chunks(AT_H + 1 + h, AT_H + 2 + h)
                chunks(AT_H + HC + 1, AT_LT + 1)

                count = [0]

                def chained(ins):
                    count[0] += 1
                    ins.then_inc(soft, 1)
                    dve.wait_ge(soft, b * SOFT + count[0])

                def bc(v):
                    return v[:].unsqueeze(2).to_broadcast([P, TPB, E])

                def row(v):
                    return v[:].unsqueeze(1).to_broadcast([P, TPB, E])

                dve.wait_ge(logits_ready, b + 1)
                chained(nc.vector.tensor_tensor(lg[:], tb[:, 0:TPB * E].rearrange("p (k e) -> p k e", e=E),
                                                row(bgb), ALU.add))
                chained(nc.vector.tensor_reduce(mx[:], lg[:], AX.X, ALU.max))
                nc.vector.tensor_tensor(zz[:], lg[:], bc(mx), ALU.subtract).then_inc(z_done, 1)
                dve.wait_ge(z_done, b + 1)
                for k in range(TPB):
                    nc_last = nc.vector.scalar_tensor_tensor(eq[:, k, :], zz[:, k, :], 0.0, rnk[:],
                                                             ALU.is_ge, ALU.mult)
                    if k < TPB - 1:
                        nc_last.then_inc(eq_done, 1)
                chained(nc_last)
                dve.wait_ge(eq_done, b * (TPB - 1) + (TPB - 1))
                chained(nc.vector.tensor_reduce(fi[:], eq[:], AX.X, ALU.max))
                chained(nc.vector.tensor_tensor(eq[:], eq[:], bc(fi), ALU.is_equal))
                dve.wait_ge(tanh_done, b + 1)
                chained(nc.vector.tensor_scalar(dn[:], th[:], -1.0, 1.0, ALU.mult, ALU.add))
                chained(nc.vector.reciprocal(dn[:], dn[:]))
                chained(nc.vector.scalar_tensor_tensor(ex[:].rearrange("p a b -> p (a b)"),
                                                       th[:].rearrange("p a b -> p (a b)"), 1.0,
                                                       dn[:].rearrange("p a b -> p (a b)"),
                                                       ALU.add, ALU.mult))
                chained(nc.vector.tensor_reduce(sm[:], ex[:], AX.X, ALU.add))
                chained(nc.vector.reciprocal(pr[:], sm[:]))
                assert count[0] == SOFT
                nc.vector.tensor_tensor(cf[:], eq[:], bc(pr), ALU.mult).then_inc(coef_done, 1)
                chunks(AT_LT + 1, AT_BD + 2)
                dve.wait_ge(bd_ready, b + 1)
                nc.vector.tensor_tensor(x1[:], x1[:], tb[:].rearrange("p (k c) -> p k c", c=C), ALU.add
                                        ).then_inc(bd_done, 1)
                dve.wait_ge(bd_done, b + 1)
                for k in range(TPB):
                    chunks(AT_BD + 2 if k == 0 else AT_Y + Y_STEP * (k - 1) + 2, AT_Y + Y_STEP * k + 2)
                    dve.wait_ge(y_ready, b * TPB + (k + 1))
                    for e in range(E):
                        ins = nc.vector.scalar_tensor_tensor(
                            x1[:, k, :], yb[e // 4][:, (e % 4) * C:(e % 4 + 1) * C], cf[:, k, e:e + 1],
                            x1[:, k, :], ALU.mult, ALU.add)
                        if e < E - 1:
                            ins.then_inc(comb, 1)
                            dve.wait_ge(comb, b * (TPB * (E - 1)) + (k * (E - 1) + e + 1))
                    ins.then_inc(y_used, 1)
                chunks(AT_Y + Y_STEP * (TPB - 1) + 2, CHUNKS)

            step(0, 1, True)
            with dve.Fori(1, BLOCKS - 1) as b:
                step(b, b + 1)
            step(BLOCKS - 1, None)

        @block.tensor
        def _(pe):
            def products(B, c, first=False):
                if c == 0 and not first:
                    pe.wait_ge(relu_done, B)
                pe.wait_ge(adj_lo, B * CHUNKS + (c + 1))
                for q in range(JB):
                    j = c * JB + q
                    for n, (wt, a) in enumerate(((xw_hi, a_hi), (xw_hi, a_lo), (xw_lo, a_hi))):
                        mm = nc.tensor.matmul(agg[:], wt[:, j, :], a[:, c % RING, q, :],
                                              start=(j == 0 and n == 0), stop=(j == TILES - 1 and n == 2))
                mm.then_inc(adj_mm, 1)

            def setup(g):
                for u in range(2):
                    pe.wait_ge(su_xn, g * GT + (u + 1) * TPB)
                    for v in range(TPB):
                        src = x1[:, v, :] if u else h_f[:].rearrange("p a (b c) -> p (a b) c", c=C)[:, v, :]
                        t = nc.tensor.transpose(hb[u][:, v * P:(v + 1) * P], src, idn[:])
                    t.then_inc(su_tr, 1)
                for u in range(2):
                    pe.wait_ge(su_xt, 2 * g + u + 1)
                    if g:
                        pe.wait_ge(su_lo, 2 * g + u - 1)
                    for v in range(TPB):
                        mm = nc.tensor.matmul(yb[u][:, v * C:(v + 1) * C], x_t[:, u, v * P:(v + 1) * P],
                                              wagg[:], start=True, stop=True)
                    mm.then_inc(su_xw, 1)

            pe.wait_ge(small_in, 16 * 8)
            setup(0)
            for c in range(CHUNKS):
                g = c // CPG
                if c % CPG == 0:
                    pe.wait_ge(su_lo, 2 * g + 2)
                products(0, c, True)
                if c % CPG == 0 and g + 1 < GROUPS:
                    setup(g + 1)
            pe.wait_ge(w_lo, 1 + 2 * HC)

            def step(b, B):
                def chunks(lo, hi):
                    if B is not None:
                        for c in range(lo, hi):
                            products(B, c)

                chunks(0, AT_X1T)
                pe.wait_ge(relu_done, b + 1)
                for k in range(TPB):
                    t = nc.tensor.transpose(tb[:, k * P:(k + 1) * P], relu_t[:, k * P:(k + 1) * P], idn[:])
                t.then_inc(x1t_ready, 1)
                chunks(AT_X1T, AT_XNT)
                for k in range(TPB):
                    pe.wait_ge(xn_done, b * TPB + (k + 1))
                    t = nc.tensor.transpose(tb[:, k * P:(k + 1) * P], xn2[:, k * P:(k + 1) * P], idn[:])
                t.then_inc(xnt_ready, 1)
                chunks(AT_XNT, AT_H)

                def router(h):
                    pe.wait_ge(gelu_done, b * HC + (h + 1))
                    nc.tensor.matmul(lb[0:E, :], wg[:, h, :], h_f[:, h % 2, :], start=(h == 0),
                                     stop=(h == HC - 1)).then_inc(logit_mm, 1)

                for h in range(HC):
                    if h == 0:
                        pe.wait_ge(xnt_lo_done, b + 1)
                    if h >= 2:
                        pe.wait_ge(gelu_done, b * HC + (h - 1))
                    for n, (wt, a) in enumerate(((w1_hi, xnt_hi), (w1_hi, xnt_lo), (w1_lo, xnt_hi))):
                        mm = nc.tensor.matmul(hb[h % 2][:], wt[:, h * P:(h + 1) * P], a[:],
                                              start=(n == 0), stop=(n == 2))
                    mm.then_inc(h_ready, 1)
                    chunks(AT_H + h, AT_H + h + 1)
                    if h >= 1:
                        router(h - 1)
                router(HC - 1)
                chunks(AT_H + HC, AT_LT)
                pe.wait_ge(lt_done, b + 1)
                for k in range(TPB):
                    t = nc.tensor.matmul(tb[:, k * E:(k + 1) * E], lct[:, k * P:(k + 1) * P], idn[0:E, 0:E],
                                         start=True, stop=True)
                t.then_inc(logits_ready, 1)
                chunks(AT_LT, AT_CT)
                pe.wait_ge(coef_done, b + 1)
                for k in range(TPB):
                    t = nc.tensor.transpose(zb[0:E, k * P:(k + 1) * P], cf[:, k, :], idn[:])
                t.then_inc(ct_ready, 1)
                chunks(AT_CT, AT_BD)
                pe.wait_ge(ct_done, b + 1)
                for k in range(TPB):
                    mm = nc.tensor.matmul(tb[:, k * C:(k + 1) * C], lct[:, k * P:(k + 1) * P], bdr[:],
                                          start=True, stop=True)
                mm.then_inc(bd_ready, 1)
                chunks(AT_BD, AT_Y)
                pe.wait_ge(h_lo_done, b * HC + HC)
                for k in range(TPB):
                    if k:
                        pe.wait_ge(y_used, b * TPB + k)
                    for h in range(HC):
                        for n, (a, wt) in enumerate(((h_hi, wd_hi), (h_hi, wd_lo), (h_lo, wd_hi))):
                            for u in range(2):
                                mm = nc.tensor.matmul(yb[u][:], a[:, h, k * P:(k + 1) * P],
                                                      wt[:, h, u * BLOCK:(u + 1) * BLOCK],
                                                      start=(h == 0 and n == 0), stop=(h == HC - 1 and n == 2))
                    mm.then_inc(y_ready, 1)
                    chunks(AT_Y + Y_STEP * k, AT_Y + Y_STEP * (k + 1) if k < TPB - 1 else CHUNKS)

            step(0, 1)
            with pe.Fori(1, BLOCKS - 1) as b:
                step(b, b + 1)
            step(BLOCKS - 1, None)


def kernel(x, adj, L0_gnn_w, L0_gnn_W_agg, L0_ffn_W1, L0_ffn_b1, L0_ffn_Wg, L0_ffn_bg, L0_ffn_Wd, L0_ffn_bd):
    import numpy as np
    import concourse.bacc as bacc
    from concourse.bass_utils import run_bass_kernel_spmd

    a = np.asarray
    arrays = {
        "x": a(x).reshape(TILES, P, C).transpose(1, 0, 2),
        "adj": a(adj).reshape(BLOCKS, BLOCK, CHUNKS, JB, P).transpose(0, 2, 4, 3, 1),
        "w": a(L0_gnn_w).reshape(TILES, P).T,
        "W_agg": a(L0_gnn_W_agg),
        "W1": a(L0_ffn_W1),
        "b1": a(L0_ffn_b1).reshape(HC, P).T,
        "Wg": a(L0_ffn_Wg).reshape(HC, P, E).transpose(1, 0, 2),
        "bg": np.broadcast_to(a(L0_ffn_bg), (P, E)),
        "Wd": a(L0_ffn_Wd).reshape(E, HC, P, C).transpose(1, 2, 0, 3).reshape(HC, P, E * C),
        "bd": a(L0_ffn_bd),
        "ident": np.eye(P, dtype=np.float32),
        "rank": np.broadcast_to(np.arange(E, 0, -1, dtype=np.float32), (P, E)),
    }
    arrays = {f"in_{k}": np.ascontiguousarray(v) for k, v in arrays.items()}
    nc = bacc.Bacc("TRN2", target_bir_lowering=False, num_devices=1)
    args = [nc.dram_tensor(k, v.shape, F32, kind="ExternalInput").ap() for k, v in arrays.items()]
    out = nc.dram_tensor("out_x", (BLOCKS, P, TPB, C), F32, kind="ExternalOutput").ap()
    build(nc, *args, out)
    r = run_bass_kernel_spmd(nc, [arrays], core_ids=[0])
    got = r.results[0]["out_x"]
    return np.ascontiguousarray(got.transpose(0, 2, 1, 3)).reshape(N, C)
```

```python
from contextlib import ExitStack

import concourse.bass as bass
from concourse import mybir

F32 = mybir.dt.float32
F32R = mybir.dt.float32r
ALU = mybir.AluOpType
ACT = mybir.ActivationFunctionType
AX = mybir.AxisListType

P = 128
N = 8192
C = 128
HID = 512
E = 8
BLOCK = 512
BLOCKS = N // BLOCK
TILES = N // P
TPB = BLOCK // P
JB = 2
CHUNKS = TILES // JB
RAW = 8
RING = 4
HC = HID // P
UNITS = BLOCKS
CPU = TPB // JB
WAVE = 3
EPS = 1e-5

PE_XNT, PE_H, PE_LT, PE_Y, PE_CT, PE_BD = 4, 7, 12, 13, 15, 17
ACT_RELU, ACT_XNT, ACT_H, ACT_LT, ACT_TANH, ACT_CT = 2, 6, 9, 13, 15, 17
DVE_X1, DVE_AGGR, DVE_XN, DVE_XNT, DVE_H, DVE_SOFT, DVE_BD = 2, 3, 5, 7, 10, 14, 19
DVE_Y = (20, 23, 26, 30)
W_STEP = 8


def build(nc, x, adj, w, W_agg, W1, b1, Wg, bg, Wd, bd, ident, rank, out):
    with ExitStack() as ctx:
        def sb(name, shape, dt=F32):
            return ctx.enter_context(nc.sbuf_tensor(name, shape, dt))

        def bank(name):
            return ctx.enter_context(nc.psum_tensor(name, [P, BLOCK], F32))

        def sem(name):
            return ctx.enter_context(nc.semaphore(name))

        xw_hi = sb("xw_hi", [P, TILES, C], F32R)
        xw_lo = sb("xw_lo", [P, TILES, C], F32R)
        wd_hi = sb("wd_hi", [P, HC, E * C], F32R)
        wd_lo = sb("wd_lo", [P, HC, E * C], F32R)
        w1_hi = sb("w1_hi", [P, HID], F32R)
        w1_lo = sb("w1_lo", [P, HID], F32R)
        wagg = sb("wagg", [P, C])
        wg = sb("wg", [P, HC, E])
        b1c = sb("b1c", [P, HC])
        bgb = sb("bgb", [P, E])
        bdr = sb("bdr", [E, C])
        idn = sb("idn", [P, P])
        rnk = sb("rnk", [P, E])
        wcol = sb("wcol", [P, TILES])
        s = sb("s", [P, TILES])
        mv1 = sb("mv1", [P, TILES, 2])
        rs1 = sb("rs1", [P, TILES])
        skip_a = sb("skip_a", [P, TILES])
        skip_b = sb("skip_b", [P, TILES])
        expo = sb("expo", [P, TPB])
        eps = sb("eps", [P, TPB])
        raw = sb("raw", [P, RAW, JB, BLOCK])
        a_hi = sb("a_hi", [P, RING, JB, BLOCK], F32R)
        a_lo = sb("a_lo", [P, RING, JB, BLOCK], F32R)
        xb = sb("xb", [P, 2, TPB, C])
        h_f = sb("h_f", [P, 2, BLOCK])
        tmp = sb("tmp", [P, 2, BLOCK])
        x1 = sb("x1", [P, TPB, C])
        rows = sb("rows", [P, TPB, C])
        xnt_hi = sb("xnt_hi", [P, BLOCK], F32R)
        xnt_lo = sb("xnt_lo", [P, BLOCK], F32R)
        h_hi = sb("h_hi", [P, HC, BLOCK], F32R)
        h_lo = sb("h_lo", [P, HC, BLOCK], F32R)
        lct = sb("lct", [E, BLOCK])
        st = sb("st", [P, 2, TPB, 6])
        mv = sb("mv", [P, TPB, 2])
        veps = sb("veps", [P, TPB])
        rstd = sb("rstd", [P, TPB])
        lg = sb("lg", [P, TPB, E])
        zz = sb("zz", [P, TPB, E])
        th = sb("th", [P, TPB, E])
        dn = sb("dn", [P, TPB, E])
        ex = sb("ex", [P, TPB, E])
        eq = sb("eq", [P, TPB, E])
        cf = sb("cf", [P, TPB, E])
        mx = sb("mx", [P, TPB])
        sm = sb("sm", [P, TPB])
        pr = sb("pr", [P, TPB])
        fi = sb("fi", [P, TPB])

        agg = bank("agg")
        tb = bank("tb")
        hb = [bank("hb0"), bank("hb1")]
        yb = [bank("yb0"), bank("yb1")]
        lb = bank("lb")
        zb = bank("zb")
        y_banks = [yb, hb]

        relu_t, xn2 = tmp[:, 0, :], tmp[:, 1, :]
        stage = [x1[:].rearrange("p a b -> p (a b)"), rows[:].rearrange("p a b -> p (a b)")]
        pieces = [(W1, w1_hi[:], w1_lo[:])] + [
            (Wd[h, :, u * BLOCK:(u + 1) * BLOCK], wd_hi[:, h, u * BLOCK:(u + 1) * BLOCK],
             wd_lo[:, h, u * BLOCK:(u + 1) * BLOCK])
            for h in range(HC) for u in range(2)]
        smalls = [(wcol, w), (wagg, W_agg), (idn, ident), (wg, Wg), (b1c, b1), (bgb, bg), (bdr, bd),
                  (rnk, rank)]

        small_in = sem("small_in")
        consts_done = sem("consts_done")
        s_done = sem("s_done")
        x_in = [sem(f"x_in{i}") for i in range(2)]
        su_st = sem("su_st")
        su_mv = sem("su_mv")
        su_veps = sem("su_veps")
        su_rstd = sem("su_rstd")
        su_xn = sem("su_xn")
        su_tr = sem("su_tr")
        su_xt = sem("su_xt")
        su_xw = sem("su_xw")
        su_hi = sem("su_hi")
        su_lo = sem("su_lo")
        su_skip = sem("su_skip")
        w_in = [sem(f"w_in{i}") for i in range(2)]
        w_hi = sem("w_hi")
        w_lo = sem("w_lo")
        raw_in = [sem(f"raw_in{r}") for r in range(RAW)]
        adj_hi = sem("adj_hi")
        adj_lo = sem("adj_lo")
        adj_mm = sem("adj_mm")
        relu_done = sem("relu_done")
        x1t_ready = sem("x1t_ready")
        skip_done = sem("skip_done")
        x1_done = sem("x1_done")
        st_done = sem("st_done")
        mv_done = sem("mv_done")
        veps_done = sem("veps_done")
        rstd_done = sem("rstd_done")
        xn_done = sem("xn_done")
        xnt_ready = sem("xnt_ready")
        xnt_hi_done = sem("xnt_hi_done")
        xnt_lo_done = sem("xnt_lo_done")
        h_ready = sem("h_ready")
        gelu_done = sem("gelu_done")
        h_hi_done = sem("h_hi_done")
        h_lo_done = sem("h_lo_done")
        logit_mm = sem("logit_mm")
        lt_done = sem("lt_done")
        logits_ready = sem("logits_ready")
        z_done = sem("z_done")
        tanh_done = sem("tanh_done")
        soft = sem("soft")
        coef_done = sem("coef_done")
        ct_ready = sem("ct_ready")
        ct_done = sem("ct_done")
        bd_ready = sem("bd_ready")
        bd_done = sem("bd_done")
        y_ready = sem("y_ready")
        comb = sem("comb")
        y_used = sem("y_used")
        out_done = sem("out_done")
        SOFT = 11
        COMB = TPB * (E - 1)

        block = ctx.enter_context(nc.Block())

        @block.sync
        def _(sp):
            def load(B, c):
                nc.sync.dma_start(raw[:, c % RAW], adj[B, c]).then_inc(raw_in[c % RAW], 16)

            for n in range(UNITS):
                if n >= 2:
                    sp.wait_ge(su_xn, (n - 1) * TPB)
                nc.sync.dma_start(xb[:, n % 2], x[:, n]).then_inc(x_in[n % 2], 16)
                for c in range(n * CPU, (n + 1) * CPU):
                    if c >= RAW:
                        sp.wait_ge(adj_lo, c - RAW + 1)
                    load(0, c)
            sp.wait_ge(su_xn, (UNITS - 1) * TPB)
            nc.sync.dma_start(xb[:, 0], x[:, 0]).then_inc(x_in[0], 16)
            with sp.Fori(1, BLOCKS) as B:
                for c in range(CHUNKS):
                    sp.wait_ge(adj_lo, B * CHUNKS + (c - RAW + 1))
                    load(B, c)
                    if c == CHUNKS // 2:
                        sp.wait_ge(x1_done, B * TPB)
                        nc.sync.dma_start(xb[:, 0], x[:, bass.ds(B, 1)].rearrange("p a t c -> p (a t) c")
                                          ).then_inc(x_in[0], 16)

        @block.gpsimd
        def _(pool):
            nc.gpsimd.memset(expo[:], -0.5).then_inc(consts_done, 1)
            nc.gpsimd.memset(eps[:], EPS).then_inc(consts_done, 1)
            pool.wait_ge(consts_done, 2)
            for n in range(UNITS):
                t0 = n * TPB
                pool.wait_ge(su_mv, (n + 1) * TPB)
                nc.gpsimd.tensor_tensor(rs1[:, t0:t0 + TPB], mv1[:, t0:t0 + TPB, 1], eps[:], ALU.add
                                        ).then_inc(su_veps, 1)
                pool.wait_ge(su_veps, n + 1)
                nc.gpsimd.tensor_tensor(rs1[:, t0:t0 + TPB], rs1[:, t0:t0 + TPB], expo[:], ALU.pow
                                        ).then_inc(su_rstd, 1)
                m = n - W_STEP + 2
                if 0 <= m < len(pieces):
                    if m >= 2:
                        pool.wait_ge(w_lo, m - 1)
                    nc.gpsimd.dma_start(stage[m % 2], pieces[m][0]).then_inc(w_in[m % 2], 16)

            def step(b):
                pool.wait_ge(mv_done, b * TPB + TPB)
                nc.gpsimd.tensor_tensor(veps[:], mv[:, :, 1], eps[:], ALU.add).then_inc(veps_done, 1)
                pool.wait_ge(veps_done, b + 1)
                nc.gpsimd.tensor_tensor(rstd[:], veps[:], expo[:], ALU.pow).then_inc(rstd_done, 1)
                pool.wait_ge(y_used, b * TPB + TPB)
                nc.gpsimd.dma_start(out[b], rows[:]).then_inc(out_done, 16)

            step(0)
            with pool.Fori(1, BLOCKS) as b:
                step(b)
            pool.wait_ge(out_done, 16 * BLOCKS)

        @block.scalar
        def _(act):
            for dst, src in smalls:
                nc.scalar.dma_start(dst[:], src).then_inc(small_in, 16)
            act.wait_ge(small_in, 16 * len(smalls))
            nc.scalar.activation(s[:], wcol[:], ACT.Sigmoid).then_inc(s_done, 1)

            def split(B, c, first=False):
                act.wait_ge(raw_in[c % RAW], B * (16 * CHUNKS // RAW) + 16 * (c // RAW + 1))
                if not (first and c < RING):
                    act.wait_ge(adj_mm, B * CHUNKS + (c - RING + 1))
                nc.scalar.activation(a_hi[:, c % RING], raw[:, c % RAW], ACT.Copy).then_inc(adj_hi, 1)

            for n in range(UNITS + WAVE):
                if n >= WAVE:
                    for c in range((n - WAVE) * CPU, (n - WAVE + 1) * CPU):
                        split(0, c, True)
                if 1 <= n <= UNITS:
                    act.wait_ge(su_tr, n)
                    if n >= 3:
                        act.wait_ge(su_xw, n - 2)
                    nc.scalar.copy(tmp[:, (n - 1) % 2, :], hb[(n - 1) % 2][:]).then_inc(su_xt, 1)
                if 2 <= n <= UNITS + 1:
                    t0 = (n - 2) * TPB
                    act.wait_ge(su_xw, n - 1)
                    nc.scalar.activation(xw_hi[:, t0:t0 + TPB, :], yb[n % 2][:], ACT.Copy).then_inc(su_hi, 1)
                m = n - W_STEP
                if 0 <= m < len(pieces):
                    act.wait_ge(w_in[m % 2], 16 * (m // 2 + 1))
                    nc.scalar.activation(pieces[m][1], stage[m % 2], ACT.Copy).then_inc(w_hi, 1)

            def step(b, B):
                for c in range(CHUNKS):
                    if B is not None:
                        split(B, c)
                    if c == ACT_RELU:
                        act.wait_ge(adj_mm, b * CHUNKS + CHUNKS)
                        nc.scalar.activation(relu_t, agg[:], ACT.Relu).then_inc(relu_done, 1)
                    if c == ACT_XNT:
                        act.wait_ge(xnt_ready, b + 1)
                        nc.scalar.activation(xnt_hi[:], tb[:], ACT.Copy).then_inc(xnt_hi_done, 1)
                    if ACT_H <= c < ACT_H + HC:
                        h = c - ACT_H
                        act.wait_ge(h_ready, b * HC + (h + 1))
                        if h >= 2:
                            act.wait_ge(h_lo_done, b * HC + (h - 1))
                            act.wait_ge(logit_mm, b * HC + (h - 1))
                        nc.scalar.activation(h_f[:, h % 2, :], hb[h % 2][:], ACT.Gelu,
                                             bias=b1c[:, h:h + 1]).then_inc(gelu_done, 1)
                        act.wait_ge(gelu_done, b * HC + (h + 1))
                        nc.scalar.activation(h_hi[:, h, :], h_f[:, h % 2, :], ACT.Copy
                                             ).then_inc(h_hi_done, 1)
                    if c == ACT_LT:
                        act.wait_ge(logit_mm, b * HC + HC)
                        nc.scalar.copy(lct[:], lb[0:E, :]).then_inc(lt_done, 1)
                    if c == ACT_TANH:
                        act.wait_ge(z_done, b + 1)
                        nc.scalar.activation(th[:], zz[:], ACT.Tanh, scale=0.5).then_inc(tanh_done, 1)
                    if c == ACT_CT:
                        act.wait_ge(ct_ready, b + 1)
                        nc.scalar.copy(lct[:], zb[0:E, :]).then_inc(ct_done, 1)

            step(0, 1)
            with act.Fori(1, BLOCKS - 1) as b:
                step(b, b + 1)
            step(BLOCKS - 1, None)

        @block.vector
        def _(dve):
            def split(B, c):
                dve.wait_ge(adj_hi, B * CHUNKS + (c + 1))
                nc.vector.tensor_tensor(a_lo[:, c % RING], raw[:, c % RAW], a_hi[:, c % RING].bitcast(F32),
                                        ALU.subtract).then_inc(adj_lo, 1)

            for n in range(UNITS + WAVE):
                if n >= WAVE:
                    v = n - WAVE
                    dve.wait_ge(su_hi, v + 1)
                    nc.vector.tensor_tensor(xw_lo[:, v * TPB:(v + 1) * TPB, :],
                                            yb[v % 2][:].rearrange("p (a b) -> p a b", b=C),
                                            xw_hi[:, v * TPB:(v + 1) * TPB, :].bitcast(F32),
                                            ALU.subtract).then_inc(su_lo, 1)
                    split(0, v * CPU)
                if 1 <= n <= UNITS:
                    v = n - 1
                    dve.wait_ge(su_rstd, n)
                    if n >= 3:
                        dve.wait_ge(su_tr, n - 2)
                    for t in range(TPB):
                        i = v * TPB + t
                        nc.vector.tensor_scalar(h_f[:, v % 2, t * C:(t + 1) * C], xb[:, v % 2, t, :],
                                                mv1[:, i, 0:1], rs1[:, i:i + 1], ALU.subtract, ALU.mult
                                                ).then_inc(su_xn, 1)
                if n >= WAVE:
                    split(0, (n - WAVE) * CPU + 1)
                if n < UNITS:
                    dve.wait_ge(x_in[n % 2], 16 * (n // 2 + 1))
                    for t in range(TPB):
                        nc.vector.bn_stats(st[:, n % 2, t, :], xb[:, n % 2, t, :]).then_inc(su_st, 1)
                    for t in range(TPB):
                        dve.wait_ge(su_st, n * TPB + t + 1)
                        nc.vector.bn_aggr(mv1[:, n * TPB + t, :], st[:, n % 2, t, :]).then_inc(su_mv, 1)
                m = n - W_STEP
                if 0 <= m < len(pieces):
                    dve.wait_ge(w_hi, m + 1)
                    nc.vector.tensor_tensor(pieces[m][2], stage[m % 2], pieces[m][1].bitcast(F32),
                                            ALU.subtract).then_inc(w_lo, 1)
            dve.wait_ge(s_done, 1)
            dve.wait_ge(su_rstd, UNITS)
            steps = [0]

            def one(ins):
                steps[0] += 1
                ins.then_inc(su_skip, 1)
                dve.wait_ge(su_skip, steps[0])

            one(nc.vector.tensor_scalar(skip_a[:], s[:], -1.0, 1.0, ALU.mult, ALU.add))
            one(nc.vector.tensor_tensor(skip_a[:], skip_a[:], rs1[:], ALU.mult))
            one(nc.vector.scalar_tensor_tensor(skip_b[:], mv1[:, :, 0], -1.0, skip_a[:], ALU.mult, ALU.mult))
            one(nc.vector.tensor_scalar(skip_a[:], skip_a[:], 1.0, None, ALU.add))

            def bc(v):
                return v[:].unsqueeze(2).to_broadcast([P, TPB, E])

            def row(v):
                return v[:].unsqueeze(1).to_broadcast([P, TPB, E])

            def step(b, B, first=False):
                for c in range(CHUNKS):
                    if c == 0:
                        dve.wait_ge(x_in[0], b * 16 + 16 * (UNITS // 2 + 1))
                        for k in range(TPB):
                            nc.vector.tensor_scalar(xb[:, 0, k, :], xb[:, 0, k, :],
                                                    skip_a[:, bass.ds(b * TPB + k, 1)],
                                                    skip_b[:, bass.ds(b * TPB + k, 1)],
                                                    ALU.mult, ALU.add).then_inc(skip_done, 1)
                    if B is not None:
                        split(B, c)
                    if c == DVE_X1:
                        dve.wait_ge(x1t_ready, b + 1)
                        for k in range(TPB):
                            if k == 0:
                                dve.wait_ge(skip_done, b * TPB + TPB)
                            nc.vector.scalar_tensor_tensor(
                                x1[:, k, :], tb[:, k * C:(k + 1) * C], s[:, bass.ds(b * TPB + k, 1)],
                                xb[:, 0, k, :], ALU.mult, ALU.add).then_inc(x1_done, 1)
                        for k in range(TPB):
                            dve.wait_ge(x1_done, b * TPB + (k + 1))
                            nc.vector.bn_stats(st[:, 0, k, :], x1[:, k, :]).then_inc(st_done, 1)
                        dve.wait_ge(st_done, b * TPB + TPB)
                    if c == DVE_AGGR:
                        for k in range(TPB):
                            nc.vector.bn_aggr(mv[:, k, :], st[:, 0, k, :]).then_inc(mv_done, 1)
                    if c == DVE_XN:
                        dve.wait_ge(rstd_done, b + 1)
                        for k in range(TPB):
                            nc.vector.tensor_scalar(xn2[:, k * C:(k + 1) * C], x1[:, k, :], mv[:, k, 0:1],
                                                    rstd[:, k:k + 1], ALU.subtract, ALU.mult
                                                    ).then_inc(xn_done, 1)
                    if c == DVE_XNT:
                        dve.wait_ge(xnt_hi_done, b + 1)
                        nc.vector.tensor_tensor(xnt_lo[:], tb[:], xnt_hi[:].bitcast(F32), ALU.subtract
                                                ).then_inc(xnt_lo_done, 1)
                    if DVE_H <= c < DVE_H + HC:
                        h = c - DVE_H
                        dve.wait_ge(h_hi_done, b * HC + (h + 1))
                        nc.vector.tensor_tensor(h_lo[:, h, :], h_f[:, h % 2, :], h_hi[:, h, :].bitcast(F32),
                                                ALU.subtract).then_inc(h_lo_done, 1)
                    if c == DVE_SOFT:
                        count = [0]

                        def chained(ins, wait=True):
                            count[0] += 1
                            ins.then_inc(soft, 1)
                            if wait:
                                dve.wait_ge(soft, b * SOFT + count[0])

                        dve.wait_ge(logits_ready, b + 1)
                        chained(nc.vector.tensor_tensor(
                            lg[:], tb[:, 0:TPB * E].rearrange("p (k e) -> p k e", e=E), row(bgb), ALU.add))
                        chained(nc.vector.tensor_reduce(mx[:], lg[:], AX.X, ALU.max))
                        nc.vector.tensor_tensor(zz[:], lg[:], bc(mx), ALU.subtract).then_inc(z_done, 1)
                        dve.wait_ge(z_done, b + 1)
                        chained(nc.vector.tensor_scalar(eq[:], zz[:], 0.0, None, ALU.is_ge))
                        chained(nc.vector.tensor_tensor(eq[:], eq[:], row(rnk), ALU.mult))
                        chained(nc.vector.tensor_reduce(fi[:], eq[:], AX.X, ALU.max))
                        chained(nc.vector.tensor_tensor(eq[:], eq[:], bc(fi), ALU.is_equal), wait=False)
                        dve.wait_ge(tanh_done, b + 1)
                        chained(nc.vector.tensor_scalar(dn[:], th[:], -1.0, 1.0, ALU.mult, ALU.add))
                        chained(nc.vector.reciprocal(dn[:], dn[:]))
                        chained(nc.vector.scalar_tensor_tensor(
                            ex[:].rearrange("p a b -> p (a b)"), th[:].rearrange("p a b -> p (a b)"), 1.0,
                            dn[:].rearrange("p a b -> p (a b)"), ALU.add, ALU.mult))
                        chained(nc.vector.tensor_reduce(sm[:], ex[:], AX.X, ALU.add))
                        chained(nc.vector.reciprocal(pr[:], sm[:]))
                        assert count[0] == SOFT
                        nc.vector.tensor_tensor(cf[:], eq[:], bc(pr), ALU.mult).then_inc(coef_done, 1)
                    if c == DVE_BD:
                        dve.wait_ge(bd_ready, b + 1)
                        nc.vector.tensor_tensor(x1[:], x1[:], tb[:].rearrange("p (k c) -> p k c", c=C),
                                                ALU.add).then_inc(bd_done, 1)
                        dve.wait_ge(bd_done, b + 1)
                        if not first:
                            dve.wait_ge(out_done, b * 16)
                    if c in DVE_Y:
                        k = DVE_Y.index(c)
                        dve.wait_ge(y_ready, b * TPB + (k + 1))
                        for e in range(E):
                            y = y_banks[k % 2][e // 4]
                            ins = nc.vector.scalar_tensor_tensor(
                                rows[:, k, :], y[:, (e % 4) * C:(e % 4 + 1) * C], cf[:, k, e:e + 1],
                                rows[:, k, :] if e else x1[:, k, :], ALU.mult, ALU.add)
                            if e < E - 1:
                                ins.then_inc(comb, 1)
                                dve.wait_ge(comb, b * COMB + (k * (E - 1) + e + 1))
                        ins.then_inc(y_used, 1)

            step(0, 1, True)
            with dve.Fori(1, BLOCKS - 1) as b:
                step(b, b + 1)
            step(BLOCKS - 1, None)

        @block.tensor
        def _(pe):
            def products(B, c):
                pe.wait_ge(adj_lo, B * CHUNKS + (c + 1))
                for q in range(JB):
                    j = c * JB + q
                    for n, (wt, a) in enumerate(((xw_hi, a_hi), (xw_hi, a_lo), (xw_lo, a_hi))):
                        mm = nc.tensor.matmul(agg[:], wt[:, j, :], a[:, c % RING, q, :],
                                              start=(j == 0 and n == 0), stop=(j == TILES - 1 and n == 2))
                mm.then_inc(adj_mm, 1)

            pe.wait_ge(small_in, 16 * len(smalls))
            for n in range(UNITS + WAVE):
                if 1 <= n <= UNITS:
                    v = n - 1
                    pe.wait_ge(su_xn, n * TPB)
                    if n >= 3:
                        pe.wait_ge(su_xt, n - 2)
                    for t in range(TPB):
                        mm = nc.tensor.transpose(hb[v % 2][:, t * P:(t + 1) * P],
                                                 h_f[:, v % 2, t * C:(t + 1) * C], idn[:])
                    mm.then_inc(su_tr, 1)
                if 2 <= n <= UNITS + 1:
                    v = n - 2
                    pe.wait_ge(su_xt, v + 1)
                    if v >= 2:
                        pe.wait_ge(su_lo, v - 1)
                    for t in range(TPB):
                        mm = nc.tensor.matmul(yb[v % 2][:, t * C:(t + 1) * C], tmp[:, v % 2, t * P:(t + 1) * P],
                                              wagg[:], start=True, stop=True)
                    mm.then_inc(su_xw, 1)
                if n >= WAVE:
                    pe.wait_ge(su_lo, n - WAVE + 1)
                    for c in range((n - WAVE) * CPU, (n - WAVE + 1) * CPU):
                        products(0, c)
            pe.wait_ge(w_lo, len(pieces))

            def router(b, h):
                pe.wait_ge(gelu_done, b * HC + (h + 1))
                nc.tensor.matmul(lb[0:E, :], wg[:, h, :], h_f[:, h % 2, :], start=(h == 0),
                                 stop=(h == HC - 1)).then_inc(logit_mm, 1)

            def step(b, B):
                pe.wait_ge(relu_done, b + 1)
                for k in range(TPB):
                    t = nc.tensor.transpose(tb[:, k * P:(k + 1) * P], relu_t[:, k * P:(k + 1) * P], idn[:])
                t.then_inc(x1t_ready, 1)
                for c in range(CHUNKS):
                    if B is not None:
                        products(B, c)
                    if c == PE_XNT:
                        for k in range(TPB):
                            pe.wait_ge(xn_done, b * TPB + (k + 1))
                            t = nc.tensor.transpose(tb[:, k * P:(k + 1) * P], xn2[:, k * P:(k + 1) * P], idn[:])
                        t.then_inc(xnt_ready, 1)
                    if PE_H <= c < PE_H + HC:
                        h = c - PE_H
                        if h == 0:
                            pe.wait_ge(xnt_lo_done, b + 1)
                        if h >= 2:
                            pe.wait_ge(gelu_done, b * HC + (h - 1))
                        for n, (wt, a) in enumerate(((w1_hi, xnt_hi), (w1_hi, xnt_lo), (w1_lo, xnt_hi))):
                            mm = nc.tensor.matmul(hb[h % 2][:], wt[:, h * P:(h + 1) * P], a[:],
                                                  start=(n == 0), stop=(n == 2))
                        mm.then_inc(h_ready, 1)
                    if PE_H < c <= PE_H + HC:
                        router(b, c - PE_H - 1)
                    if c == PE_LT:
                        pe.wait_ge(lt_done, b + 1)
                        for k in range(TPB):
                            t = nc.tensor.matmul(tb[:, k * E:(k + 1) * E], lct[:, k * P:(k + 1) * P],
                                                 idn[0:E, 0:E], start=True, stop=True)
                        t.then_inc(logits_ready, 1)
                    if c == PE_CT:
                        pe.wait_ge(coef_done, b + 1)
                        for k in range(TPB):
                            t = nc.tensor.transpose(zb[0:E, k * P:(k + 1) * P], cf[:, k, :], idn[:])
                        t.then_inc(ct_ready, 1)
                    if c == PE_BD:
                        pe.wait_ge(ct_done, b + 1)
                        for k in range(TPB):
                            mm = nc.tensor.matmul(tb[:, k * C:(k + 1) * C], lct[:, k * P:(k + 1) * P], bdr[:],
                                                  start=True, stop=True)
                        mm.then_inc(bd_ready, 1)
                    if PE_Y <= c < PE_Y + TPB * HC:
                        k, h = divmod(c - PE_Y, HC)
                        if k == 0:
                            pe.wait_ge(h_lo_done, b * HC + (h + 1))
                        if h == 0 and k >= 2:
                            pe.wait_ge(y_used, b * TPB + (k - 1))
                        for n, (a, wt) in enumerate(((h_hi, wd_hi), (h_hi, wd_lo), (h_lo, wd_hi))):
                            for u in range(2):
                                mm = nc.tensor.matmul(y_banks[k % 2][u][:], a[:, h, k * P:(k + 1) * P],
                                                      wt[:, h, u * BLOCK:(u + 1) * BLOCK],
                                                      start=(h == 0 and n == 0), stop=(h == HC - 1 and n == 2))
                        if h == HC - 1:
                            mm.then_inc(y_ready, 1)

            step(0, 1)
            with pe.Fori(1, BLOCKS - 1) as b:
                step(b, b + 1)
            step(BLOCKS - 1, None)


def kernel(x, adj, L0_gnn_w, L0_gnn_W_agg, L0_ffn_W1, L0_ffn_b1, L0_ffn_Wg, L0_ffn_bg, L0_ffn_Wd, L0_ffn_bd):
    import numpy as np
    import concourse.bacc as bacc
    from concourse.bass_utils import run_bass_kernel_spmd

    a = np.asarray
    arrays = {
        "x": a(x).reshape(BLOCKS, TPB, P, C).transpose(2, 0, 1, 3),
        "adj": a(adj).reshape(BLOCKS, BLOCK, CHUNKS, JB, P).transpose(0, 2, 4, 3, 1),
        "w": a(L0_gnn_w).reshape(TILES, P).T,
        "W_agg": a(L0_gnn_W_agg),
        "W1": a(L0_ffn_W1),
        "b1": a(L0_ffn_b1).reshape(HC, P).T,
        "Wg": a(L0_ffn_Wg).reshape(HC, P, E).transpose(1, 0, 2),
        "bg": np.broadcast_to(a(L0_ffn_bg), (P, E)),
        "Wd": a(L0_ffn_Wd).reshape(E, HC, P, C).transpose(1, 2, 0, 3).reshape(HC, P, E * C),
        "bd": a(L0_ffn_bd),
        "ident": np.eye(P, dtype=np.float32),
        "rank": np.broadcast_to(np.arange(E, 0, -1, dtype=np.float32), (P, E)),
    }
    arrays = {f"in_{k}": np.ascontiguousarray(v) for k, v in arrays.items()}
    nc = bacc.Bacc("TRN2", target_bir_lowering=False, num_devices=1)
    args = [nc.dram_tensor(k, v.shape, F32, kind="ExternalInput").ap() for k, v in arrays.items()]
    out = nc.dram_tensor("out_x", (BLOCKS, P, TPB, C), F32, kind="ExternalOutput").ap()
    build(nc, *args, out)
    r = run_bass_kernel_spmd(nc, [arrays], core_ids=[0])
    got = r.results[0]["out_x"]
    return np.ascontiguousarray(got.transpose(0, 2, 1, 3)).reshape(N, C)
```

```python
from contextlib import ExitStack

import concourse.bass as bass
from concourse import mybir

F32 = mybir.dt.float32
F32R = mybir.dt.float32r
I32 = mybir.dt.int32
ALU = mybir.AluOpType
ACT = mybir.ActivationFunctionType
AX = mybir.AxisListType

P = 128
N = 8192
C = 128
HID = 512
E = 8
BLOCK = 512
BLOCKS = N // BLOCK
TILES = N // P
TPB = BLOCK // P
JB = 2
CHUNKS = TILES // JB
RAW = 4
RING = 4
HC = HID // P
UNITS = BLOCKS
CPU = TPB // JB
WAVE = 3
EPS = 1e-5
REC = 2 * C + 8
BP = 4
PARTS = BLOCKS // BP
PT = BP * TPB
REGION = PT * P + P
ET = PT + E
ROWS = E * REGION
GT = 4
EG = ET // GT
assert EG == 2 * (BP - 1)
DONE = EG * (PARTS - 1)
OUT_RING = 4
TAIL_RECS = 4

PE_XNT = 7
PE_H = 10
PE_RANK = 17
ACT_RELU = 1
ACT_XNT = 10
ACT_H = 13
ACT_TANH = 19
DVE_X1 = 2
DVE_AGGR = 3
DVE_XN = 6
DVE_XNT = 11
DVE_SOFT = 18
DVE_POS = 22
PE_T = (0, 16)
PE_EH = (2, 19)
PE_Y = (8, 25)
ACT_T = (3, 20)
ACT_EH = (6, 23)
DVE_T = (3, 20)
DVE_EH = (6, 23)
DVE_SUM = (10, 28)
SP_REC = (0, 13)
LATE = 10
LATE_Y = 11
DVE_TAB = 10
TAB_STAGES = 6
SP_ZERO = 14
SP_OUT = 12
DVE_LN = 2
W_STEP = 2
W_AT = 6
EXP0 = BP + 1


def build(nc, x, adj, w, W_agg, W1, b1, Wg, bg, Wd, bd, ident, rank, before, starts, tiles, out):
    with ExitStack() as ctx:
        def sb(name, shape, dt=F32):
            return ctx.enter_context(nc.sbuf_tensor(name, shape, dt))

        def bank(name):
            return ctx.enter_context(nc.psum_tensor(name, [P, BLOCK], F32))

        def sem(name):
            return ctx.enter_context(nc.semaphore(name))

        xw_hi = sb("xw_hi", [P, TILES, C], F32R)
        xw_lo = sb("xw_lo", [P, TILES, C], F32R)
        wd = sb("wd", [P, HC, E, 2, C], F32R)
        w1_hi = sb("w1_hi", [P, HID], F32R)
        w1_lo = sb("w1_lo", [P, HID], F32R)
        wagg = sb("wagg", [P, C])
        wg = sb("wg", [P, HC, E])
        b1c = sb("b1c", [P, HC])
        bgb = sb("bgb", [P, E])
        bdb = sb("bdb", [P, E * C])
        idn = sb("idn", [P, P])
        rnk = sb("rnk", [P, E])
        low_ones = sb("low_ones", [P, P])
        ones = sb("ones", [P, P])
        starts_sb = sb("starts_sb", [P, E])
        run = sb("run", [P, E])
        pos = sb("pos", [P, TILES])
        pos_b = sb("pos_b", [P, TPB], I32)
        pos_i = sb("pos_i", [P, TILES], I32)
        inc = sb("inc", [P, E - 1])
        move = sb("move", [P, PT, E - 1])
        shift = sb("shift", [P, PT])
        turn = sb("turn", [P, 1])
        zrec = sb("zrec", [P, REC])
        wcol = sb("wcol", [P, TILES])
        s = sb("s", [P, TILES])
        mv1 = sb("mv1", [P, TILES, 2])
        rs1 = sb("rs1", [P, TILES])
        skip_a = sb("skip_a", [P, TILES])
        skip_b = sb("skip_b", [P, TILES])
        expo = sb("expo", [P, TPB])
        eps = sb("eps", [P, TPB])
        raw = sb("raw", [P, RAW, JB, BLOCK])
        a_hi = sb("a_hi", [P, RING, JB, BLOCK], F32R)
        a_lo = sb("a_lo", [P, RING, JB, BLOCK], F32R)
        xb = sb("xb", [P, 2, TPB, C])
        h_f = sb("h_f", [P, 2, BLOCK])
        tmp = sb("tmp", [P, 2, BLOCK])
        rec = sb("rec", [P, TPB, REC])
        stage = sb("stage", [P, 2, BLOCK])
        xnt_hi = sb("xnt_hi", [P, BLOCK], F32R)
        xnt_lo = sb("xnt_lo", [P, BLOCK], F32R)
        st = sb("st", [P, 2, TPB, 6])
        mv = sb("mv", [P, TPB, 2])
        veps = sb("veps", [P, TPB])
        rstd = sb("rstd", [P, TPB])
        lg = sb("lg", [P, TPB, E])
        zz = sb("zz", [P, TPB, E])
        th = sb("th", [P, TPB, E])
        dn = sb("dn", [P, TPB, E])
        ex = sb("ex", [P, TPB, E])
        eq = sb("eq", [P, TPB + 1, E])
        pp = sb("pp", [P, TPB, E])
        mx = sb("mx", [P, TPB])
        sm = sb("sm", [P, TPB])
        fi = sb("fi", [P, TPB])
        pf = sb("pf", [P, TPB])
        cnt = sb("cnt", [P, E])
        nti = sb("nti", [P, E], I32)
        nt = sb("nt", [P, E])
        cum = sb("cum", [1, 2, 2 * E])
        tvec = sb("tvec", [1, ET])
        tv = sb("tv", [1, ET])
        cmp = sb("cmp", [1, ET, E])
        et = sb("et", [1, ET])
        ft = sb("ft", [1, ET])
        row0 = sb("row0", [1, PARTS * ET], I32)
        ecol = sb("ecol", [1, PARTS * ET], I32)
        wcols = sb("wcols", [1, PARTS * ET], I32)
        fill = sb("fill", [1, PARTS * E], I32)
        recs0 = sb("recs0", [P, GT, REC])
        hh0 = sb("hh0", [P, HC, BLOCK], F32R)
        hl0 = sb("hl0", [P, HC, BLOCK], F32R)

        eh_f = stage
        outs = tmp[:, 1, :].rearrange("p (k c) -> p k c", c=C)
        ysum0 = xb[:, 1]
        raw_flat = raw[:].rearrange("p a b c -> p (a b c)")
        o = (TAIL_RECS - 1) * GT * REC
        recs = [recs0[:]] + [raw_flat[:, i * GT * REC:(i + 1) * GT * REC].rearrange("p (k c) -> p k c", k=GT)
                             for i in range(TAIL_RECS - 1)]
        ysum = [ysum0, raw_flat[:, o:o + GT * C].rearrange("p (k c) -> p k c", k=GT)]
        outs_last = raw_flat[:, 0:PT * C].rearrange("p (k c) -> p k c", c=C)
        h_hi = [hh0[:], a_hi[:].rearrange("p a b c -> p (a b) c")[:, 0:HC, :]]
        h_lo = [hl0[:], a_lo[:].rearrange("p a b c -> p (a b) c")[:, 0:HC, :]]
        table = [nc.dram_tensor(f"records{q}", (ROWS, REC), F32).ap() for q in range(PARTS)]
        results = [nc.dram_tensor(f"results{q}", (ET * P, C), F32).ap() for q in range(PARTS)]

        agg = bank("agg")
        tb = bank("tb")
        hb = [bank("hb0"), bank("hb1")]
        yb = [bank("yb0"), bank("yb1")]
        lb = bank("lb")
        etb = bank("etb")

        relu_t = tmp[:, 0, :]
        pieces = [(W1, w1_hi[:], w1_lo[:])] + [
            (Wd[h, :, u * BLOCK:(u + 1) * BLOCK], wd[:, h, u * BLOCK // C:(u + 1) * BLOCK // C, 0, :],
             wd[:, h, u * BLOCK // C:(u + 1) * BLOCK // C, 1, :])
            for h in range(HC) for u in range(E * C // BLOCK)]

        def like(v, m):
            return v if m == 0 else v.rearrange("p (e c) -> p e c", c=C)

        wd_flat = wd[:].rearrange("p h e s c -> p h (e s c)")
        smalls = [(wcol, w), (wagg, W_agg), (idn, ident), (wg, Wg), (b1c, b1), (bgb, bg), (bdb, bd),
                  (rnk, rank), (low_ones, before), (starts_sb, starts), (run, starts), (tvec, tiles)]

        small_in = sem("small_in")
        consts_done = sem("consts_done")
        s_done = sem("s_done")
        x_in = [sem(f"x_in{i}") for i in range(2)]
        su_st = sem("su_st")
        su_mv = sem("su_mv")
        su_veps = sem("su_veps")
        su_rstd = sem("su_rstd")
        su_xn = sem("su_xn")
        su_xn_pool = sem("su_xn_pool")
        su_tr = sem("su_tr")
        su_xt = sem("su_xt")
        su_xw = sem("su_xw")
        su_hi = sem("su_hi")
        su_lo = sem("su_lo")
        su_skip = sem("su_skip")
        w_in = [sem(f"w_in{i}") for i in range(2)]
        w_hi = sem("w_hi")
        w_lo = sem("w_lo")
        raw_in = [sem(f"raw_in{r}") for r in range(RAW)]
        adj_hi = sem("adj_hi")
        adj_lo = sem("adj_lo")
        adj_mm = sem("adj_mm")
        relu_done = sem("relu_done")
        x1t_ready = sem("x1t_ready")
        skip_done = sem("skip_done")
        x1_done = sem("x1_done")
        st_done = sem("st_done")
        mv_done = sem("mv_done")
        veps_done = sem("veps_done")
        rstd_done = sem("rstd_done")
        xn_done = sem("xn_done")
        xnt_ready = sem("xnt_ready")
        xnt_hi_done = sem("xnt_hi_done")
        xnt_lo_done = sem("xnt_lo_done")
        h_ready = sem("h_ready")
        gelu_done = sem("gelu_done")
        logit_mm = sem("logit_mm")
        z_done = sem("z_done")
        tanh_done = sem("tanh_done")
        soft = sem("soft")
        eq_done = sem("eq_done")
        rank_ready = sem("rank_ready")
        pos_done = sem("pos_done")
        pos_kept = sem("pos_kept")
        res_pos = sem("res_pos")
        turned = sem("turned")
        rec_out = sem("rec_out")
        SOFT = 14
        tab = sem("tab")
        fill_done = sem("fill_done")
        tab_done = sem("tab_done")
        filled = sem("filled")
        filled_pool = sem("filled_pool")
        rec_in = [sem(f"rec_in{i}") for i in range(TAIL_RECS)]
        ex_tr = sem("ex_tr")
        ex_xhi = sem("ex_xhi")
        ex_xlo = sem("ex_xlo")
        ex_h = sem("ex_h")
        ex_gelu = sem("ex_gelu")
        ex_hhi = sem("ex_hhi")
        ex_hlo = sem("ex_hlo")
        ex_y = sem("ex_y")
        ex_bd = sem("ex_bd")
        ex_sum = sem("ex_sum")
        res_out = [sem(f"res_out{i}") for i in range(2)]
        out_in = [sem(f"out_in{i}") for i in range(OUT_RING)]
        out_done = [sem(f"out_done{i}") for i in range(OUT_RING)]
        last_in = [sem(f"last_in{i}") for i in range(BP)]
        last_done = sem("last_done")

        segments = []
        for q in range(PARTS):
            end = (q + 1) * BP - (q == PARTS - 1)
            segments += [(q * BP, q * BP + 1), (q * BP + 1, end)]
        segments.append((BLOCKS - 1, BLOCKS))

        def groups_of(b, lo):
            q = lo // BP - 1
            if q < 0 or lo % BP == 0:
                return None
            return b * 2 + (q * EG - 2 * ((q + 1) * BP + 1))

        def is_step(b, n):
            return isinstance(b, int) and b == n

        def zero_rows(engine, dma, signal, q, e):
            i = q * E + e
            at = engine.value_load(fill[0:1, i:i + 1], min_val=e * REGION, max_val=e * REGION + PT * P)
            dma.dma_start(table[q][bass.ds(at, P), :], zrec[:]).then_inc(signal, 16)

        def slot_of(t):
            return (t + 1) % TAIL_RECS, t % 2

        block = ctx.enter_context(nc.Block())

        @block.sync
        def _(sp):
            def load(B, c):
                nc.sync.dma_start(raw[:, c % RAW], adj[B, c]).then_inc(raw_in[c % RAW], 16)

            for n in range(UNITS + 1):
                if n < UNITS:
                    if n >= 2:
                        sp.wait_ge(su_xn, (n - 1) * DVE_LN)
                        sp.wait_ge(su_xn_pool, (n - 1) * (TPB - DVE_LN))
                    nc.sync.dma_start(xb[:, n % 2], x[:, n]).then_inc(x_in[n % 2], 16)
                for c in range(max(n - 1, 0) * CPU, n * CPU):
                    if c >= RAW:
                        sp.wait_ge(adj_lo, c - RAW + 1)
                    load(0, c)
            sp.wait_ge(su_xn, (UNITS - 1) * DVE_LN)
            sp.wait_ge(su_xn_pool, (UNITS - 1) * (TPB - DVE_LN))
            nc.sync.dma_start(xb[:, 0], x[:, 0]).then_inc(x_in[0], 16)

            def load_tile(g, k, q, slot=0):
                at = sp.value_load(row0[0:1, bass.ds(g * GT + k, 1)], min_val=0, max_val=ROWS - P)
                nc.sync.dma_start(recs[slot][:, k, :], table[q][bass.ds(at, P), :]).then_inc(rec_in[slot], 16)

            def put(q, t):
                i = q * PT + t
                sp.wait_ge(out_in[t % OUT_RING], 16 * (i // OUT_RING + 1))
                nc.sync.dma_start(out[i], outs[:, t % OUT_RING, :]).then_inc(out_done[t % OUT_RING], 16)

            def step(b, due, part, g):
                B = b + 1
                last = is_step(b, BLOCKS - 1)
                for c in range(CHUNKS):
                    if not last:
                        sp.wait_ge(adj_lo, B * CHUNKS + (c - RAW + 1))
                        load(B, c)
                        if c == CHUNKS // 2:
                            sp.wait_ge(x1_done, B * TPB)
                            if isinstance(b, int):
                                nc.sync.dma_start(xb[:, 0], x[:, B]).then_inc(x_in[0], 16)
                            else:
                                nc.sync.dma_start(xb[:, 0], x[:, bass.ds(B, 1)].rearrange("p a t c -> p (a t) c")
                                                  ).then_inc(x_in[0], 16)
                    if due is not None:
                        if SP_ZERO <= c < SP_ZERO + E:
                            if c == SP_ZERO:
                                sp.wait_ge(fill_done, due + 1)
                                sp.wait_ge(rec_out, 16 * PT * (due + 1))
                            zero_rows(sp, nc.sync, filled, due, c - SP_ZERO)
                        if due >= 1 and SP_OUT <= c < SP_OUT + PT:
                            put(due - 1, c - SP_OUT)
                    if g is not None:
                        for i in range(2):
                            if SP_REC[i] <= c < SP_REC[i] + GT:
                                k = c - SP_REC[i]
                                if not (isinstance(g, int) and g + i == 0):
                                    sp.wait_ge(ex_sum, (g + i) * GT + (k + 1 - GT))
                                load_tile(g + i, k, part)

            for lo, end in segments:
                q = lo // BP - 1
                if lo == EXP0:
                    step(lo, None, q, 0)
                    lo += 1
                if lo % BP == 0:
                    step(lo, q if q >= 0 else None, None, None)
                    if q >= 0:
                        sp.wait_ge(filled, 16 * E * (q + 1))
                        sp.wait_ge(tab_done, q + 1)
                elif end - lo == 1:
                    step(lo, None, q, groups_of(lo, lo))
                else:
                    with sp.Fori(lo, end) as b:
                        step(b, None, q, groups_of(b, lo))

            q = PARTS - 1
            sp.wait_ge(fill_done, q + 1)
            ats = [sp.value_load(fill[0:1, q * E + e:q * E + e + 1], min_val=e * REGION, max_val=e * REGION + PT * P)
                   for e in range(E // 2)]
            sp.wait_ge(rec_out, 16 * PT * (q + 1))
            for at in ats:
                nc.sync.dma_start(table[q][bass.ds(at, P), :], zrec[:]).then_inc(filled, 16)
            sp.wait_ge(tab_done, q + 1)
            sp.wait_ge(filled, 16 * E * q + 16 * (E // 2))
            sp.wait_ge(filled_pool, 16 * (E // 2))
            for t in range(EG):
                slot, _ = slot_of(t)
                if t < TAIL_RECS and slot == 0:
                    sp.wait_ge(ex_sum, DONE * GT)
                if t >= TAIL_RECS:
                    sp.wait_ge(ex_sum, (DONE + t - TAIL_RECS + 1) * GT)
                for k in range(GT):
                    load_tile(DONE + t, k, q, slot)
            for t in range(PT):
                put(q - 1, t)
            by_block = out.rearrange("(g k) p c -> g p k c", k=TPB)
            for i in range(BP):
                sp.wait_ge(last_in[i], 16 * TPB)
                nc.sync.dma_start(by_block[q * BP + i], outs_last[:, i * TPB:(i + 1) * TPB, :]
                                  ).then_inc(last_done, 16)
            sp.wait_ge(last_done, 16 * BP)
            for r in range(OUT_RING):
                sp.wait_ge(out_done[r], 16 * (PT * (PARTS - 1) // OUT_RING))

        @block.gpsimd
        def _(pool):
            nc.gpsimd.memset(expo[:], -0.5).then_inc(consts_done, 1)
            nc.gpsimd.memset(eps[:], EPS).then_inc(consts_done, 1)
            nc.gpsimd.memset(ones[:], 1.0).then_inc(consts_done, 1)
            nc.gpsimd.memset(zrec[:], 0.0).then_inc(consts_done, 1)
            nc.gpsimd.memset(eq[:], 0.0).then_inc(consts_done, 1)
            nc.gpsimd.memset(rec[:], 0.0).then_inc(consts_done, 1)
            nc.gpsimd.memset(cum[:], 0.0).then_inc(consts_done, 1)
            pool.wait_ge(consts_done, 7)

            def carry(signal, value, before):
                if before is not None:
                    pool.wait_ge(turned, before)
                pool.wait_ge(signal, value)
                nc.gpsimd.tensor_tensor(turn[:], eps[:, 0:1], eps[:, 0:1], ALU.add).then_inc(turned, 1)

            def weights_in(m):
                if m >= 2:
                    pool.wait_ge(w_lo, m - 1)
                nc.gpsimd.dma_start(stage[:, m % 2, :], pieces[m][0]).then_inc(w_in[m % 2], 16)

            for n in range(UNITS):
                t0 = n * TPB
                pool.wait_ge(su_mv, (n + 1) * TPB)
                nc.gpsimd.tensor_tensor(rs1[:, t0:t0 + TPB], mv1[:, t0:t0 + TPB, 1], eps[:], ALU.add
                                        ).then_inc(su_veps, 1)
                pool.wait_ge(su_veps, n + 1)
                nc.gpsimd.tensor_tensor(rs1[:, t0:t0 + TPB], rs1[:, t0:t0 + TPB], expo[:], ALU.pow
                                        ).then_inc(su_rstd, 1)
                pool.wait_ge(su_rstd, n + 1)
                if n >= 2:
                    pool.wait_ge(su_tr, n - 1)
                for t in range(DVE_LN, TPB):
                    i = t0 + t
                    nc.gpsimd.tensor_scalar(h_f[:, n % 2, t * C:(t + 1) * C], xb[:, n % 2, t, :],
                                            mv1[:, i, 0:1], rs1[:, i:i + 1], ALU.subtract, ALU.mult
                                            ).then_inc(su_xn_pool, 1)
                if n == W_STEP:
                    weights_in(0)
                    weights_in(1)

            def take(q, t):
                i = q * PT + t
                if i >= OUT_RING:
                    pool.wait_ge(out_done[t % OUT_RING], 16 * (i // OUT_RING))
                nc.gpsimd.indirect_dma_start(
                    outs[:, t % OUT_RING, :], None, results[q][:, :],
                    bass.IndirectOffsetOnAxis(ap=pos_i[:, i:i + 1], axis=0)).then_inc(out_in[t % OUT_RING], 16)

            def give(q, g, n, slot=0):
                pool.wait_ge(ex_sum, n * GT + GT)
                by_group = results[q][:, :].rearrange("(g k p) c -> g p k c", p=P, k=GT)
                if isinstance(g, int):
                    dst = by_group[g]
                else:
                    dst = by_group[bass.ds(g, 1)].rearrange("a p k c -> (a p) k c")
                nc.gpsimd.dma_start(dst, ysum[slot]).then_inc(res_out[slot], 16)

            def step(b, q, due=None, g=None):
                first = is_step(b, 0)
                last = is_step(b, BLOCKS - 1)
                pool.wait_ge(mv_done, b * TPB + TPB)
                nc.gpsimd.tensor_tensor(veps[:], mv[:, :, 1], eps[:], ALU.add).then_inc(veps_done, 1)
                pool.wait_ge(veps_done, b + 1)
                nc.gpsimd.tensor_tensor(rstd[:], veps[:], expo[:], ALU.pow).then_inc(rstd_done, 1)
                if first:
                    for m in range(2, len(pieces)):
                        weights_in(m)
                if due is not None and due >= 1:
                    pool.wait_ge(res_out[0], 16 * EG * due)
                    pool.wait_ge(res_pos, due)
                    for t in range(PT):
                        take(due - 1, t)
                pool.wait_ge(pos_done, b + 1)
                for k in range(TPB):
                    if not first or k:
                        carry(rec_out, b * (16 * TPB) + 16 * k, None if first and k == 1 else b * TPB + (k - 1))
                    nc.gpsimd.indirect_dma_start(
                        table[q][:, :], bass.IndirectOffsetOnAxis(ap=pos_b[:, k:k + 1], axis=0), rec[:, k, :], None
                    ).then_inc(rec_out, 16)
                    if g is not None and k == 0 and not last:
                        give(q - 1, g - (q - 1) * EG, g)
                if last:
                    pool.wait_ge(fill_done, q + 1)
                    pool.wait_ge(rec_out, 16 * PT * (q + 1))
                    for e in range(E // 2, E):
                        zero_rows(pool, nc.gpsimd, filled_pool, q, e)
                    give(q - 1, g - (q - 1) * EG, g)
                if g is not None:
                    give(q - 1, g + (1 - (q - 1) * EG), g + 1)

            for lo, end in segments:
                q = lo // BP
                if end - lo == 1:
                    step(lo, q, q - 1 if q and lo % BP == 0 else None, groups_of(lo, lo))
                else:
                    with pool.Fori(lo, end) as b:
                        step(b, q, None, groups_of(b, lo))

            q = PARTS - 1
            pool.wait_ge(res_out[0], 16 * EG * q)
            pool.wait_ge(res_pos, q)
            for t in range(EG):
                give(q, t, DONE + t, slot_of(t)[1])
                if t < EG - 1:
                    for i in range(t * PT // (EG - 1), (t + 1) * PT // (EG - 1)):
                        take(q - 1, i)
            pool.wait_ge(res_out[0], 16 * (DONE + EG // 2))
            pool.wait_ge(res_out[1], 16 * (EG // 2))
            pool.wait_ge(res_pos, PARTS)
            for t in range(PT):
                nc.gpsimd.indirect_dma_start(
                    outs_last[:, t, :], None, results[q][:, :],
                    bass.IndirectOffsetOnAxis(ap=pos_i[:, q * PT + t:q * PT + t + 1], axis=0)
                ).then_inc(last_in[t // TPB], 16)

        @block.scalar
        def _(act):
            for dst, src in smalls:
                nc.scalar.dma_start(dst[:], src).then_inc(small_in, 16)
            act.wait_ge(small_in, 16 * len(smalls))
            nc.scalar.activation(s[:], wcol[:], ACT.Sigmoid).then_inc(s_done, 1)

            def split(B, c, first=False):
                act.wait_ge(raw_in[c % RAW], B * (16 * CHUNKS // RAW) + 16 * (c // RAW + 1))
                if not (first and c < RING):
                    act.wait_ge(adj_mm, B * CHUNKS + (c - RING + 1))
                nc.scalar.activation(a_hi[:, c % RING], raw[:, c % RAW], ACT.Copy).then_inc(adj_hi, 1)

            def weights_high(m):
                act.wait_ge(w_in[m % 2], 16 * (m // 2 + 1))
                nc.scalar.activation(pieces[m][1], like(stage[:, m % 2, :], m), ACT.Copy).then_inc(w_hi, 1)

            for n in range(UNITS + WAVE):
                if n >= WAVE:
                    for c in range((n - WAVE) * CPU, (n - WAVE + 1) * CPU):
                        split(0, c, True)
                if 2 <= n <= UNITS + 1:
                    t0 = (n - 2) * TPB
                    act.wait_ge(su_xw, n - 1)
                    nc.scalar.activation(xw_hi[:, t0:t0 + TPB, :], yb[n % 2][:], ACT.Copy).then_inc(su_hi, 1)
                if 1 <= n <= UNITS:
                    act.wait_ge(su_tr, n)
                    if n >= 3:
                        act.wait_ge(su_xw, n - 2)
                    nc.scalar.copy(tmp[:, (n - 1) % 2, :], hb[(n - 1) % 2][:]).then_inc(su_xt, 1)
                if n == W_STEP + 2:
                    weights_high(0)

            def ex_rows(g):
                act.wait_ge(ex_tr, g + 1)
                nc.scalar.activation(xnt_hi[:], etb[:], ACT.Copy).then_inc(ex_xhi, 1)

            def ex_gelu_of(g, h, slot=0, used=None):
                act.wait_ge(ex_h, g * HC + (h + 1))
                if not (isinstance(g, int) and g * HC + h < 2):
                    act.wait_ge(ex_hlo, g * HC + (h - 1))
                nc.scalar.activation(eh_f[:, h % 2, :], hb[h % 2][:], ACT.Gelu, bias=b1c[:, h:h + 1]
                                     ).then_inc(ex_gelu, 1)
                if h == 0 and used is not None:
                    act.wait_ge(ex_y, used * GT)
                act.wait_ge(ex_gelu, g * HC + (h + 1))
                nc.scalar.activation(h_hi[slot][:, h, :], eh_f[:, h % 2, :], ACT.Copy).then_inc(ex_hhi, 1)

            def step(b, B, g=None):
                late = 0 if B is not None else LATE
                for c in range(CHUNKS + late):
                    if B is not None:
                        split(B, c)
                    m = (c - W_AT) // 2
                    if is_step(b, 0) and 1 <= m < len(pieces) and (c - W_AT) % 2 == 0:
                        weights_high(m)
                    if c == ACT_RELU:
                        act.wait_ge(adj_mm, b * CHUNKS + CHUNKS)
                        nc.scalar.activation(relu_t, agg[:], ACT.Relu).then_inc(relu_done, 1)
                    if c == ACT_XNT:
                        act.wait_ge(xnt_ready, b + 1)
                        nc.scalar.activation(xnt_hi[:], tb[:], ACT.Copy).then_inc(xnt_hi_done, 1)
                    if ACT_H <= c < ACT_H + HC:
                        h = c - ACT_H
                        act.wait_ge(h_ready, b * HC + (h + 1))
                        if h >= 2:
                            act.wait_ge(logit_mm, b * HC + (h - 1))
                        nc.scalar.activation(h_f[:, h % 2, :], hb[h % 2][:], ACT.Gelu,
                                             bias=b1c[:, h:h + 1]).then_inc(gelu_done, 1)
                    if c == ACT_TANH:
                        act.wait_ge(z_done, b + 1)
                        nc.scalar.activation(th[:], zz[:], ACT.Tanh, scale=0.5).then_inc(tanh_done, 1)
                    if g is not None:
                        for i in range(2):
                            if c - late * i == ACT_T[i]:
                                ex_rows(g + i)
                            if ACT_EH[i] <= c - late * i < ACT_EH[i] + HC:
                                ex_gelu_of(g + i, c - late * i - ACT_EH[i], 0,
                                           None if isinstance(g, int) and g + i == 0 else g + i)

            for lo, end in segments:
                if lo == EXP0:
                    step(lo, lo + 1, 0)
                    lo += 1
                if end - lo == 1:
                    step(lo, None if lo == BLOCKS - 1 else lo + 1, groups_of(lo, lo))
                else:
                    with act.Fori(lo, end) as b:
                        step(b, b + 1, groups_of(b, lo))

            ex_rows(DONE)
            for t in range(EG):
                g, slot = DONE + t, slot_of(t)[1]
                for h in range(HC):
                    if h == HC - 1 and t + 1 < EG:
                        act.wait_ge(ex_h, (g + 1) * HC)
                        ex_rows(g + 1)
                    ex_gelu_of(g, h, slot, None if t == 1 else g if t == 0 else g - 1)

        @block.vector
        def _(dve):
            def split(B, c):
                dve.wait_ge(adj_hi, B * CHUNKS + (c + 1))
                nc.vector.tensor_tensor(a_lo[:, c % RING], raw[:, c % RAW], a_hi[:, c % RING].bitcast(F32),
                                        ALU.subtract).then_inc(adj_lo, 1)

            def weights_low(m):
                dve.wait_ge(w_hi, m + 1)
                nc.vector.tensor_tensor(pieces[m][2], like(stage[:, m % 2, :], m), pieces[m][1].bitcast(F32),
                                        ALU.subtract).then_inc(w_lo, 1)

            for n in range(UNITS + WAVE):
                if n >= WAVE:
                    v = n - WAVE
                    dve.wait_ge(su_hi, v + 1)
                    nc.vector.tensor_tensor(xw_lo[:, v * TPB:(v + 1) * TPB, :],
                                            yb[v % 2][:].rearrange("p (a b) -> p a b", b=C),
                                            xw_hi[:, v * TPB:(v + 1) * TPB, :].bitcast(F32),
                                            ALU.subtract).then_inc(su_lo, 1)
                    split(0, v * CPU)
                if 1 <= n <= UNITS:
                    v = n - 1
                    dve.wait_ge(su_rstd, n)
                    if n >= 3:
                        dve.wait_ge(su_tr, n - 2)
                    for t in range(DVE_LN):
                        i = v * TPB + t
                        nc.vector.tensor_scalar(h_f[:, v % 2, t * C:(t + 1) * C], xb[:, v % 2, t, :],
                                                mv1[:, i, 0:1], rs1[:, i:i + 1], ALU.subtract, ALU.mult
                                                ).then_inc(su_xn, 1)
                if n >= WAVE:
                    split(0, (n - WAVE) * CPU + 1)
                if n < UNITS:
                    dve.wait_ge(x_in[n % 2], 16 * (n // 2 + 1))
                    for t in range(TPB):
                        nc.vector.bn_stats(st[:, n % 2, t, :], xb[:, n % 2, t, :]).then_inc(su_st, 1)
                    for t in range(TPB):
                        dve.wait_ge(su_st, n * TPB + t + 1)
                        nc.vector.bn_aggr(mv1[:, n * TPB + t, :], st[:, n % 2, t, :]).then_inc(su_mv, 1)
                if n == W_STEP + 2:
                    weights_low(0)
            dve.wait_ge(s_done, 1)
            dve.wait_ge(su_rstd, UNITS)
            steps = [0]

            def one(ins):
                steps[0] += 1
                ins.then_inc(su_skip, 1)
                dve.wait_ge(su_skip, steps[0])

            one(nc.vector.tensor_scalar(skip_a[:], s[:], -1.0, 1.0, ALU.mult, ALU.add))
            one(nc.vector.tensor_tensor(skip_a[:], skip_a[:], rs1[:], ALU.mult))
            one(nc.vector.scalar_tensor_tensor(skip_b[:], mv1[:, :, 0], -1.0, skip_a[:], ALU.mult, ALU.mult))
            one(nc.vector.tensor_scalar(skip_a[:], skip_a[:], 1.0, None, ALU.add))

            def bc(v):
                return v[:].unsqueeze(2).to_broadcast([P, TPB, E])

            def row(v):
                return v[:].unsqueeze(1).to_broadcast([P, TPB, E])

            n_tab = [0]

            def made(ins):
                n_tab[0] += 1
                ins.then_inc(tab, 1)
                dve.wait_ge(tab, n_tab[0])

            def over_e(v):
                return v.unsqueeze(2).to_broadcast([1, ET, E])

            def over_t(v):
                return v.unsqueeze(1).to_broadcast([1, ET, E])

            def over_pt(v):
                return v.unsqueeze(1).to_broadcast([P, PT, E - 1])

            def tile_table(q, i):
                cols = slice(q * ET, (q + 1) * ET)
                total = cum[:, 1, 2 * E - 1:2 * E]
                if i == 0:
                    nc.vector.tensor_copy(fill[:, q * E:(q + 1) * E], run[0:1, :]).then_inc(fill_done, 1)
                    made(nc.vector.tensor_tensor(cnt[:], run[:], starts_sb[:], ALU.subtract))
                    made(nc.vector.tensor_scalar(nti[:], cnt[:], float(P - 1), None, ALU.add))
                    made(nc.vector.tensor_scalar(nti[:], nti[:], P.bit_length() - 1, None, ALU.logical_shift_right))
                    made(nc.vector.tensor_copy(nt[:], nti[:]))
                if i == 1:
                    made(nc.vector.tensor_copy(run[:], starts_sb[:]))
                    made(nc.vector.tensor_copy(cum[:, 0, E:2 * E], nt[0:1, :]))
                    for n, d in enumerate((1, 2, 4)):
                        made(nc.vector.tensor_tensor(cum[:, (n + 1) % 2, E:2 * E], cum[:, n % 2, E:2 * E],
                                                     cum[:, n % 2, E - d:2 * E - d], ALU.add))
                if i == 2:
                    made(nc.vector.tensor_scalar(ft[:, 0:1], total, 1.0, None, ALU.subtract))
                    made(nc.vector.tensor_tensor(tv[:], tvec[:], ft[:, 0:1].to_broadcast([1, ET]), ALU.min))
                    made(nc.vector.tensor_tensor(cmp[:], over_e(tv[:]), over_t(cum[:, 1, E:2 * E]), ALU.is_ge))
                    made(nc.vector.tensor_reduce(et[:], cmp[:], AX.X, ALU.add))
                if i == 3:
                    made(nc.vector.tensor_tensor(cmp[:], cmp[:], over_t(nt[0:1, :]), ALU.mult))
                    made(nc.vector.tensor_reduce(ft[:], cmp[:], AX.X, ALU.add))
                    made(nc.vector.tensor_tensor(ft[:], tv[:], ft[:], ALU.subtract))
                    made(nc.vector.tensor_scalar(ecol[:, cols], et[:], float(C), None, ALU.mult))
                if i == 4:
                    made(nc.vector.tensor_scalar(wcols[:, cols], et[:], float(2 * C), None, ALU.mult))
                    made(nc.vector.tensor_scalar(et[:], et[:], float(REGION), None, ALU.mult))
                    nc.vector.scalar_tensor_tensor(row0[:, cols], ft[:], float(P), et[:], ALU.mult, ALU.add
                                                   ).then_inc(tab_done, 1)
                    dve.wait_ge(tab_done, q + 1)
                if i == 5:
                    part = pos[:, q * PT:(q + 1) * PT]
                    made(nc.vector.tensor_scalar(inc[:], nt[:, 0:E - 1], float(P), float(REGION),
                                                 ALU.mult, ALU.subtract))
                    made(nc.vector.tensor_tensor(move[:], part.unsqueeze(2).to_broadcast([P, PT, E - 1]),
                                                 over_pt(starts_sb[:, 1:E]), ALU.is_ge))
                    made(nc.vector.tensor_tensor(move[:], move[:], over_pt(inc[:]), ALU.mult))
                    made(nc.vector.tensor_reduce(shift[:], move[:], AX.X, ALU.add))
                    nc.vector.tensor_tensor(pos_i[:, q * PT:(q + 1) * PT], part, shift[:], ALU.add
                                            ).then_inc(res_pos, 1)

            def ex_low_rows(g):
                dve.wait_ge(ex_xhi, g + 1)
                nc.vector.tensor_tensor(xnt_lo[:], etb[:], xnt_hi[:].bitcast(F32), ALU.subtract
                                        ).then_inc(ex_xlo, 1)

            def ex_low(g, h, slot=0):
                dve.wait_ge(ex_hhi, g * HC + (h + 1))
                nc.vector.tensor_tensor(h_lo[slot][:, h, :], eh_f[:, h % 2, :], h_hi[slot][:, h, :].bitcast(F32),
                                        ALU.subtract).then_inc(ex_hlo, 1)

            def ex_sum_of(g, k, rslot=0, slot=0, written=None):
                if k == 0 and written is not None:
                    dve.wait_ge(res_out[slot], written * 16)
                at = dve.value_load(ecol[0:1, bass.ds(g * GT + k, 1)], min_val=0, max_val=(E - 1) * C)
                y = yb[k % 2]
                sums = ysum[slot][:, k, :]
                dve.wait_ge(ex_y, g * GT + (k + 1))
                nc.vector.tensor_tensor(sums, y[:, 0:C], bdb[:, bass.ds(at, C)], ALU.add).then_inc(ex_bd, 1)
                dve.wait_ge(ex_bd, g * (2 * GT) + (2 * k + 1))
                nc.vector.tensor_tensor(sums, sums, y[:, C:2 * C], ALU.add).then_inc(ex_bd, 1)
                dve.wait_ge(ex_bd, g * (2 * GT) + (2 * k + 2))
                nc.vector.scalar_tensor_tensor(sums, sums, recs[rslot][:, k, 2 * C:2 * C + 1],
                                               recs[rslot][:, k, 0:C], ALU.mult, ALU.add).then_inc(ex_sum, 1)

            def step(b, B, due, g):
                first = is_step(b, 0)
                count = [0]

                def chained(ins, wait=True):
                    count[0] += 1
                    ins.then_inc(soft, 1)
                    if wait:
                        dve.wait_ge(soft, b * SOFT + count[0])

                late = 0 if B is not None else LATE
                late_y = (0, 0) if B is not None else (LATE_Y, LATE)
                for c in range(CHUNKS + late):
                    if c == 0:
                        dve.wait_ge(x_in[0], b * 16 + 16 * (UNITS // 2 + 1))
                        for k in range(TPB):
                            nc.vector.tensor_scalar(xb[:, 0, k, :], xb[:, 0, k, :],
                                                    skip_a[:, bass.ds(b * TPB + k, 1)],
                                                    skip_b[:, bass.ds(b * TPB + k, 1)],
                                                    ALU.mult, ALU.add).then_inc(skip_done, 1)
                    if B is not None:
                        split(B, c)
                    m = (c - W_AT) // 2
                    if first and 1 <= m < len(pieces) and (c - W_AT) % 2 == 0:
                        weights_low(m)
                    if c == DVE_X1:
                        dve.wait_ge(x1t_ready, b + 1)
                        if not first:
                            dve.wait_ge(rec_out, b * (16 * TPB))
                        for k in range(TPB):
                            if k == 0:
                                dve.wait_ge(skip_done, b * TPB + TPB)
                            nc.vector.scalar_tensor_tensor(
                                rec[:, k, 0:C], tb[:, k * C:(k + 1) * C], s[:, bass.ds(b * TPB + k, 1)],
                                xb[:, 0, k, :], ALU.mult, ALU.add).then_inc(x1_done, 1)
                        for k in range(TPB):
                            dve.wait_ge(x1_done, b * TPB + (k + 1))
                            nc.vector.bn_stats(st[:, 0, k, :], rec[:, k, 0:C]).then_inc(st_done, 1)
                        dve.wait_ge(st_done, b * TPB + TPB)
                    if c == DVE_AGGR:
                        for k in range(TPB):
                            nc.vector.bn_aggr(mv[:, k, :], st[:, 0, k, :]).then_inc(mv_done, 1)
                    if c == DVE_XN:
                        dve.wait_ge(rstd_done, b + 1)
                        for k in range(TPB):
                            nc.vector.tensor_scalar(rec[:, k, C:2 * C], rec[:, k, 0:C], mv[:, k, 0:1],
                                                    rstd[:, k:k + 1], ALU.subtract, ALU.mult
                                                    ).then_inc(xn_done, 1)
                    if c == DVE_XNT:
                        dve.wait_ge(xnt_hi_done, b + 1)
                        nc.vector.tensor_tensor(xnt_lo[:], tb[:], xnt_hi[:].bitcast(F32), ALU.subtract
                                                ).then_inc(xnt_lo_done, 1)
                    if c == DVE_SOFT:
                        dve.wait_ge(logit_mm, b * HC + HC)
                        chained(nc.vector.tensor_tensor(
                            lg[:], lb[:, 0:TPB * E].rearrange("p (k e) -> p k e", e=E), row(bgb), ALU.add))
                        chained(nc.vector.tensor_reduce(mx[:], lg[:], AX.X, ALU.max))
                        nc.vector.tensor_tensor(zz[:], lg[:], bc(mx), ALU.subtract).then_inc(z_done, 1)
                        dve.wait_ge(z_done, b + 1)
                        chained(nc.vector.tensor_scalar(lg[:], zz[:], 0.0, None, ALU.is_ge))
                        chained(nc.vector.tensor_tensor(lg[:], lg[:], row(rnk), ALU.mult))
                        chained(nc.vector.tensor_reduce(fi[:], lg[:], AX.X, ALU.max))
                        nc.vector.tensor_tensor(eq[:, 0:TPB, :], lg[:], bc(fi), ALU.is_equal
                                                ).then_inc(eq_done, 1)
                        dve.wait_ge(tanh_done, b + 1)
                        chained(nc.vector.tensor_scalar(dn[:], th[:], -1.0, 1.0, ALU.mult, ALU.add))
                        chained(nc.vector.reciprocal(dn[:], dn[:]))
                        chained(nc.vector.scalar_tensor_tensor(
                            ex[:].rearrange("p a b -> p (a b)"), th[:].rearrange("p a b -> p (a b)"), 1.0,
                            dn[:].rearrange("p a b -> p (a b)"), ALU.add, ALU.mult))
                        chained(nc.vector.tensor_reduce(sm[:], ex[:], AX.X, ALU.add))
                        chained(nc.vector.reciprocal(rec[:, :, 2 * C:2 * C + 1].rearrange("p a b -> p (a b)"),
                                                     sm[:]), wait=False)
                    if g is not None:
                        for i in range(2):
                            if c - late * i == DVE_T[i]:
                                ex_low_rows(g + i)
                            if DVE_EH[i] <= c - late * i < DVE_EH[i] + HC:
                                ex_low(g + i, c - late * i - DVE_EH[i])
                            if DVE_SUM[i] <= c - late_y[i] < DVE_SUM[i] + GT:
                                ex_sum_of(g + i, c - late_y[i] - DVE_SUM[i], 0, 0,
                                          None if isinstance(g, int) and g + i == 0 else g + i)
                    if c == DVE_POS:
                        dve.wait_ge(rank_ready, b + 1)
                        ranks = tb[:, 0:(TPB + 1) * E].rearrange("p (k e) -> p k e", e=E)
                        chained(nc.vector.tensor_tensor(pp[:], ranks[:, 0:TPB, :], row(run), ALU.add))
                        chained(nc.vector.tensor_tensor(pp[:], pp[:], eq[:, 0:TPB, :], ALU.mult))
                        chained(nc.vector.tensor_reduce(pf[:], pp[:], AX.X, ALU.add))
                        chained(nc.vector.tensor_tensor(run[:], run[:], ranks[:, TPB, :], ALU.add))
                        assert count[0] == SOFT, count
                        nc.vector.tensor_copy(pos_b[:], pf[:]).then_inc(pos_done, 1)
                        nc.vector.tensor_copy(pos[:, bass.ds(b * TPB, TPB)], pf[:]).then_inc(pos_kept, 1)
                    tab_at = DVE_TAB if B is not None else DVE_POS
                    if due is not None and tab_at <= c < tab_at + TAB_STAGES:
                        if c == tab_at:
                            dve.wait_ge(pos_kept, (due + 1) * BP)
                        tile_table(due, c - tab_at)

            for lo, end in segments:
                q = lo // BP - 1
                if lo == EXP0:
                    step(lo, lo + 1, None, 0)
                    lo += 1
                if lo == BLOCKS - 1:
                    step(lo, None, PARTS - 1, groups_of(lo, lo))
                elif end - lo == 1:
                    step(lo, lo + 1, q if q >= 0 else None, None)
                else:
                    with dve.Fori(lo, end) as b:
                        step(b, b + 1, None, groups_of(b, lo))

            ex_low_rows(DONE)
            for t in range(EG + 1):
                g = DONE + t

                def low(h):
                    if t < EG:
                        ex_low(g, h, slot_of(t)[1])

                def sums(k):
                    if t >= 1:
                        u = t - 1
                        ex_sum_of(g - 1, k, slot_of(u)[0], slot_of(u)[1],
                                  None if u == 1 else DONE + u // 2 if u % 2 == 0 else u // 2)

                low(0)
                low(1)
                sums(0)
                low(2)
                sums(1)
                if t + 1 < EG:
                    ex_low_rows(g + 1)
                low(3)
                sums(2)
                sums(3)

        @block.tensor
        def _(pe):
            def products(B, c):
                pe.wait_ge(adj_lo, B * CHUNKS + (c + 1))
                for q in range(JB):
                    j = c * JB + q
                    for n, (wt, a) in enumerate(((xw_hi, a_hi), (xw_hi, a_lo), (xw_lo, a_hi))):
                        mm = nc.tensor.matmul(agg[:], wt[:, j, :], a[:, c % RING, q, :],
                                              start=(j == 0 and n == 0), stop=(j == TILES - 1 and n == 2))
                mm.then_inc(adj_mm, 1)

            pe.wait_ge(small_in, 16 * len(smalls))
            for n in range(UNITS + WAVE):
                if 2 <= n <= UNITS + 1:
                    v = n - 2
                    pe.wait_ge(su_xt, v + 1)
                    if v >= 2:
                        pe.wait_ge(su_lo, v - 1)
                    for t in range(TPB):
                        mm = nc.tensor.matmul(yb[v % 2][:, t * C:(t + 1) * C], tmp[:, v % 2, t * P:(t + 1) * P],
                                              wagg[:], start=True, stop=True)
                    mm.then_inc(su_xw, 1)
                if 1 <= n <= UNITS:
                    v = n - 1
                    pe.wait_ge(su_xn, n * DVE_LN)
                    pe.wait_ge(su_xn_pool, n * (TPB - DVE_LN))
                    if n >= 3:
                        pe.wait_ge(su_xt, n - 2)
                    for t in range(TPB):
                        mm = nc.tensor.transpose(hb[v % 2][:, t * P:(t + 1) * P],
                                                 h_f[:, v % 2, t * C:(t + 1) * C], idn[:])
                    mm.then_inc(su_tr, 1)
                if n >= WAVE:
                    pe.wait_ge(su_lo, n - WAVE + 1)
                    for c in range((n - WAVE) * CPU, (n - WAVE + 1) * CPU):
                        products(0, c)
            pe.wait_ge(w_lo, 1)

            def router(b, h):
                pe.wait_ge(gelu_done, b * HC + (h + 1))
                logits = lb[:, 0:TPB * E].rearrange("p (k e) -> p k e", e=E)
                zeros = eq[:, TPB:TPB + 1, :].to_broadcast([P, TPB, E])
                if h == 0:
                    nc.tensor.matmul(logits, ones[:], zeros, start=True, stop=False)
                for k in range(TPB):
                    mm = nc.tensor.matmul(logits[:, k, :], h_f[:, h % 2, k * P:(k + 1) * P], wg[:, h, :],
                                          start=False, stop=False, skip_group_check=True)
                if h == HC - 1:
                    mm = nc.tensor.matmul(logits, ones[:], zeros, start=False, stop=True)
                mm.then_inc(logit_mm, 1)

            def ex_rows(g, slot, loaded):
                pe.wait_ge(rec_in[slot], loaded * (16 * GT))
                if not (isinstance(g, int) and g == 0):
                    pe.wait_ge(ex_xlo, g)
                for k in range(GT):
                    mm = nc.tensor.transpose(etb[:, k * P:(k + 1) * P], recs[slot][:, k, C:2 * C], idn[:])
                mm.then_inc(ex_tr, 1)

            def ex_hidden(g, h):
                if h == 0:
                    pe.wait_ge(ex_xlo, g + 1)
                if not (isinstance(g, int) and g * HC + h < 2):
                    pe.wait_ge(ex_gelu, g * HC + (h - 1))
                for n, (wt, a) in enumerate(((w1_hi, xnt_hi), (w1_hi, xnt_lo), (w1_lo, xnt_hi))):
                    mm = nc.tensor.matmul(hb[h % 2][:], wt[:, h * P:(h + 1) * P], a[:],
                                          start=(n == 0), stop=(n == 2))
                mm.then_inc(ex_h, 1)

            def ex_products(g, k, slot=0):
                if k == 0:
                    pe.wait_ge(ex_hlo, g * HC + HC)
                if not (isinstance(g, int) and g * GT + k < 2):
                    pe.wait_ge(ex_bd, g * (2 * GT) + (2 * k - 2))
                at = pe.value_load(wcols[0:1, bass.ds(g * GT + k, 1)], min_val=0, max_val=(E - 1) * 2 * C)
                for h in range(HC):
                    for n, a in enumerate((h_hi[slot], h_lo[slot])):
                        mm = nc.tensor.matmul(yb[k % 2][:, 0:2 * C], a[:, h, k * P:(k + 1) * P],
                                              wd_flat[:, h, bass.ds(at, 2 * C)],
                                              start=(h == 0 and n == 0), stop=(h == HC - 1 and n == 1))
                mm.then_inc(ex_y, 1)

            def step(b, B, g=None):
                pe.wait_ge(relu_done, b + 1)
                for k in range(TPB):
                    t = nc.tensor.transpose(tb[:, k * P:(k + 1) * P], relu_t[:, k * P:(k + 1) * P], idn[:])
                t.then_inc(x1t_ready, 1)
                late = 0 if B is not None else LATE
                late_y = (0, 0) if B is not None else (LATE_Y, LATE)
                for c in range(CHUNKS + late):
                    if B is not None:
                        products(B, c)
                    if c == PE_XNT:
                        for k in range(TPB):
                            pe.wait_ge(xn_done, b * TPB + (k + 1))
                            t = nc.tensor.transpose(tb[:, k * P:(k + 1) * P], rec[:, k, C:2 * C], idn[:])
                        t.then_inc(xnt_ready, 1)
                    if PE_H <= c < PE_H + HC:
                        h = c - PE_H
                        if h == 0:
                            pe.wait_ge(xnt_lo_done, b + 1)
                            if late:
                                pe.wait_ge(ex_gelu, (g + 1) * HC)
                        if h >= 2:
                            pe.wait_ge(gelu_done, b * HC + (h - 1))
                        for n, (wt, a) in enumerate(((w1_hi, xnt_hi), (w1_hi, xnt_lo), (w1_lo, xnt_hi))):
                            mm = nc.tensor.matmul(hb[h % 2][:], wt[:, h * P:(h + 1) * P], a[:],
                                                  start=(n == 0), stop=(n == 2))
                        mm.then_inc(h_ready, 1)
                    if g is not None:
                        for i in range(2):
                            if c - late * i == PE_T[i]:
                                ex_rows(g + i, 0, g + (i + 1))
                            if PE_EH[i] <= c - late * i < PE_EH[i] + HC:
                                ex_hidden(g + i, c - late * i - PE_EH[i])
                            if PE_Y[i] <= c - late_y[i] < PE_Y[i] + GT:
                                ex_products(g + i, c - late_y[i] - PE_Y[i])
                    if PE_H < c <= PE_H + HC:
                        router(b, c - PE_H - 1)
                    if c == PE_RANK:
                        pe.wait_ge(eq_done, b + 1)
                        flat = eq[:].rearrange("p k e -> p (k e)")
                        zeros = eq[:, TPB:TPB + 1, :].to_broadcast([P, TPB + 1, E])
                        every = tb[:, 0:(TPB + 1) * E].rearrange("p (k e) -> p k e", e=E)
                        nc.tensor.matmul(every, ones[:], zeros, start=True, stop=False)
                        for k in range(TPB):
                            nc.tensor.matmul(every[:, k + 1:, :], ones[:],
                                             eq[:, k:k + 1, :].to_broadcast([P, TPB - k, E]),
                                             start=False, stop=False, skip_group_check=True)
                        mm = nc.tensor.matmul(tb[:, 0:(TPB + 1) * E], low_ones[:], flat, start=False, stop=True)
                        mm.then_inc(rank_ready, 1)

            for lo, end in segments:
                if lo == EXP0:
                    step(lo, lo + 1, 0)
                    lo += 1
                if end - lo == 1:
                    step(lo, None if lo == BLOCKS - 1 else lo + 1, groups_of(lo, lo))
                    if lo == 0:
                        pe.wait_ge(w_lo, len(pieces))
                    elif lo % BP == 0:
                        pe.wait_ge(tab_done, lo // BP)
                else:
                    with pe.Fori(lo, end) as b:
                        step(b, b + 1, groups_of(b, lo))

            pe.wait_ge(tab_done, PARTS)

            def rows_of(t):
                rslot = slot_of(t)[0]
                ex_rows(DONE + t, rslot, t // TAIL_RECS + (DONE + 1 if rslot == 0 else 1))

            rows_of(0)
            for t in range(EG + 1):
                g = DONE + t

                def hidden(h):
                    if t < EG:
                        ex_hidden(g, h)

                def product(k):
                    if t >= 1:
                        ex_products(g - 1, k, slot_of(t - 1)[1])

                hidden(0)
                hidden(1)
                product(0)
                hidden(2)
                product(1)
                if t + 1 < EG:
                    rows_of(t + 1)
                hidden(3)
                product(2)
                product(3)


def kernel(x, adj, L0_gnn_w, L0_gnn_W_agg, L0_ffn_W1, L0_ffn_b1, L0_ffn_Wg, L0_ffn_bg, L0_ffn_Wd, L0_ffn_bd):
    import numpy as np
    import concourse.bacc as bacc
    from concourse.bass_utils import run_bass_kernel_spmd

    a = np.asarray
    arrays = {
        "x": a(x).reshape(BLOCKS, TPB, P, C).transpose(2, 0, 1, 3),
        "adj": a(adj).reshape(BLOCKS, BLOCK, CHUNKS, JB, P).transpose(0, 2, 4, 3, 1),
        "w": a(L0_gnn_w).reshape(TILES, P).T,
        "W_agg": a(L0_gnn_W_agg),
        "W1": a(L0_ffn_W1),
        "b1": a(L0_ffn_b1).reshape(HC, P).T,
        "Wg": a(L0_ffn_Wg).reshape(HC, P, E).transpose(1, 0, 2),
        "bg": np.broadcast_to(a(L0_ffn_bg), (P, E)),
        "Wd": a(L0_ffn_Wd).reshape(E, HC, P, C).transpose(1, 2, 0, 3).reshape(HC, P, E * C),
        "bd": np.broadcast_to(a(L0_ffn_bd).reshape(E * C), (P, E * C)),
        "ident": np.eye(P, dtype=np.float32),
        "rank": np.broadcast_to(np.arange(E, 0, -1, dtype=np.float32), (P, E)),
        "before": np.triu(np.ones((P, P), np.float32), 1),
        "starts": np.broadcast_to(np.arange(E, dtype=np.float32) * REGION, (P, E)),
        "tiles": np.arange(ET, dtype=np.float32).reshape(1, ET),
    }
    arrays = {f"in_{k}": np.ascontiguousarray(v) for k, v in arrays.items()}
    nc = bacc.Bacc("TRN2", target_bir_lowering=False, num_devices=1)
    args = [nc.dram_tensor(k, v.shape, F32, kind="ExternalInput").ap() for k, v in arrays.items()]
    out = nc.dram_tensor("out_x", (TILES, P, C), F32, kind="ExternalOutput").ap()
    build(nc, *args, out)
    r = run_bass_kernel_spmd(nc, [arrays], core_ids=[0])
    got = r.results[0]["out_x"]
    return got.reshape(N, C)
```
